# Optimizing a Trainium2 kernel written in Bass

```python
import numpy as np
import jax
import jax.numpy as jnp

def _softmax(x, axis=-1):
    return jax.nn.softmax(x, axis=axis)

def _gelu(x):
    return jax.nn.gelu(x, approximate=True)

def _silu(x):
    return jax.nn.silu(x)

def _sigmoid(x):
    return jax.nn.sigmoid(x)

def _layernorm(x, axis=-1, eps=1e-05):
    m = jnp.mean(x, axis=axis, keepdims=True)
    v = jnp.var(x, axis=axis, keepdims=True)
    return (x - m) / jnp.sqrt(v + eps)

def _scatter_add(tgt, idx, src, axis=0):
    return tgt.at[idx].add(src)

def _segment_sum(src, seg, n):
    return jax.ops.segment_sum(src, seg, n)
kernel_name = 'mk_audio_tower_d1_tok_audfeat512_r4_84d023'

def setup_inputs(seed: int=0):
    np.random.seed(seed)
    _w = jnp.asarray

    def _rec_inputs():
        import jax
        import jax.numpy as jnp
        _rk = jax.random.key(seed)
        x = -0.000605797 + 1.00053 * jax.random.normal(jax.random.fold_in(_rk, 1), (64, 250, 64), jnp.float32)
        return x
    x = _rec_inputs()

    def _L0_tok_setup():
        import jax, jax.numpy as jnp
        import numpy as np
        PATCH_SIZES = [4, 8, 16]
        B, S, D, H = (32, 250, 64, 128)
        key = jax.random.key(seed)
        ks = jax.random.split(key, 8)
        inp = {'x': jax.random.normal(ks[0], (B, S, D), dtype=jnp.float32)}
        for i, p in enumerate(PATCH_SIZES):
            fan_in = p * D
            inp[f'W{i}'] = jax.random.normal(ks[1 + 2 * i], (H, fan_in), dtype=jnp.float32) / np.sqrt(fan_in).astype(np.float32)
            inp[f'b{i}'] = jax.random.normal(ks[2 + 2 * i], (H,), dtype=jnp.float32) * 0.01
        inp['pos'] = jax.random.normal(ks[7], (1, 250, H), dtype=jnp.float32)
        return inp
    _L0_tok_all = _L0_tok_setup()
    _L0_tok_in = {k: v for k, v in _L0_tok_all.items() if k in ('W0', 'b0', 'W1', 'b1', 'W2', 'b2', 'pos')}
    del _L0_tok_all

    def _L0_attn_setup():
        import jax, jax.numpy as jnp
        import numpy as np
        B, T, D = (16, 256, 128)
        C = 1024
        DC = 128
        A = 128
        P = 128
        key = jax.random.key(seed)
        ks = jax.random.split(key, 10)
        s = lambda fan_in: 1.0 / np.sqrt(fan_in)
        return {'model_embed': jax.random.normal(ks[0], (B, T, D), jnp.float32), 'context_embed': jax.random.normal(ks[1], (C, DC), jnp.float32), 'Wq': jax.random.uniform(ks[2], (D, A), jnp.float32, -s(D), s(D)), 'bq': jax.random.uniform(ks[3], (A,), jnp.float32, -s(D), s(D)), 'Wk': jax.random.uniform(ks[4], (DC, A), jnp.float32, -s(DC), s(DC)), 'bk': jax.random.uniform(ks[5], (A,), jnp.float32, -s(DC), s(DC)), 'Wv': jax.random.uniform(ks[6], (DC, A), jnp.float32, -s(DC), s(DC)), 'bv': jax.random.uniform(ks[7], (A,), jnp.float32, -s(DC), s(DC)), 'Wo': jax.random.uniform(ks[8], (A, P), jnp.float32, -s(A), s(A)), 'bo': jax.random.uniform(ks[9], (P,), jnp.float32, -s(A), s(A))}
    _L0_attn_all = _L0_attn_setup()
    _L0_attn_in = {k: v for k, v in _L0_attn_all.items() if k in ('context_embed', 'Wq', 'bq', 'Wk', 'bk', 'Wv', 'bv', 'Wo', 'bo')}
    del _L0_attn_all

    def _L0_ffn_setup():
        import jax, jax.numpy as jnp
        import numpy as np
        CAPACITY_FACTOR = 1.2
        key = jax.random.key(seed)
        k1, k2, k3 = jax.random.split(key, 3)
        B, S, D, E = (8, 1024, 128, 16)
        x = jax.random.normal(k1, (B, S, D), dtype=jnp.float32)
        switch_w = jax.random.normal(k2, (E, D), dtype=jnp.float32) * 0.02
        switch_b = jnp.zeros((E,), dtype=jnp.float32)
        expert_w = jax.random.normal(k3, (E, D, D), dtype=jnp.float32) * 0.02
        expert_b = jnp.zeros((E, D), dtype=jnp.float32)
        return {'x': x, 'switch_w': switch_w, 'switch_b': switch_b, 'expert_w': expert_w, 'expert_b': expert_b}
    _L0_ffn_all = _L0_ffn_setup()
    _L0_ffn_in = {k: v for k, v in _L0_ffn_all.items() if k in ('switch_w', 'switch_b', 'expert_w', 'expert_b')}
    del _L0_ffn_all
    return {'x': x, 'L0_tok_W0': _L0_tok_in['W0'], 'L0_tok_b0': _L0_tok_in['b0'], 'L0_tok_W1': _L0_tok_in['W1'], 'L0_tok_b1': _L0_tok_in['b1'], 'L0_tok_W2': _L0_tok_in['W2'], 'L0_tok_b2': _L0_tok_in['b2'], 'L0_tok_pos': _L0_tok_in['pos'], 'L0_attn_context_embed': _L0_attn_in['context_embed'], 'L0_attn_Wq': _L0_attn_in['Wq'], 'L0_attn_bq': _L0_attn_in['bq'], 'L0_attn_Wk': _L0_attn_in['Wk'], 'L0_attn_bk': _L0_attn_in['bk'], 'L0_attn_Wv': _L0_attn_in['Wv'], 'L0_attn_bv': _L0_attn_in['bv'], 'L0_attn_Wo': _L0_attn_in['Wo'], 'L0_attn_bo': _L0_attn_in['bo'], 'L0_ffn_switch_w': _L0_ffn_in['switch_w'], 'L0_ffn_switch_b': _L0_ffn_in['switch_b'], 'L0_ffn_expert_w': _L0_ffn_in['expert_w'], 'L0_ffn_expert_b': _L0_ffn_in['expert_b']}

def reference(x, L0_tok_W0, L0_tok_b0, L0_tok_W1, L0_tok_b1, L0_tok_W2, L0_tok_b2, L0_tok_pos, L0_attn_context_embed, L0_attn_Wq, L0_attn_bq, L0_attn_Wk, L0_attn_bk, L0_attn_Wv, L0_attn_bv, L0_attn_Wo, L0_attn_bo, L0_ffn_switch_w, L0_ffn_switch_b, L0_ffn_expert_w, L0_ffn_expert_b):
    import jax
    import jax.numpy as jnp

    def _L0_tok_ref(x, W0, b0, W1, b1, W2, b2, pos):
        import jax, jax.numpy as jnp
        import numpy as np
        PATCH_SIZES = [4, 8, 16]
        B, S, D, H = (32, 250, 64, 128)
        Ws = [W0, W1, W2]
        bs = [b0, b1, b2]
        batch, seq_len, d = x.shape
        min_len = seq_len - max(PATCH_SIZES) + 1
        embs = []
        for p, W, b in zip(PATCH_SIZES, Ws, bs):
            idx = jnp.arange(min_len)[:, None] + jnp.arange(p)[None, :]
            win = x[:, idx, :]
            Wk = W.reshape(-1, p, d)
            embs.append(jnp.einsum('blpd,hpd->blh', win, Wk) + b)
        out = jnp.stack(embs, axis=1).mean(axis=1)
        return out + pos[:, :min_len, :]

    def _L0_attn_ref(model_embed, context_embed, Wq, bq, Wk, bk, Wv, bv, Wo, bo):
        import jax, jax.numpy as jnp
        import numpy as np
        B, T, D = (16, 256, 128)
        C = 1024
        DC = 128
        A = 128
        P = 128
        q = model_embed @ Wq + bq
        k = context_embed @ Wk + bk
        v = context_embed @ Wv + bv
        scale = 1.0 / jnp.sqrt(jnp.asarray(q.shape[-1], q.dtype))
        scores = jnp.einsum('ck,btk->btc', k, q) * scale
        attn = jax.nn.softmax(scores, axis=-1)
        x = jnp.einsum('ck,btc->btk', v, attn)
        return x @ Wo + bo

    def _L0_ffn_ref(x, switch_w, switch_b, expert_w, expert_b):
        import jax, jax.numpy as jnp
        import numpy as np
        CAPACITY_FACTOR = 1.2
        B, S, D = x.shape
        E = switch_w.shape[0]
        N = B * S
        xf = x.reshape(N, D)
        logits = xf @ switch_w.T + switch_b
        probs = jax.nn.softmax(logits, axis=-1)
        route_probs = jnp.max(probs, axis=-1)
        routes = jnp.argmax(probs, axis=-1)
        oh = jax.nn.one_hot(routes, E, dtype=jnp.int32)
        pos = jnp.take_along_axis(jnp.cumsum(oh, axis=0), routes[:, None], axis=1)[:, 0] - 1
        capacity = int(CAPACITY_FACTOR * N / E)
        keep = pos < capacity
        buf = jnp.zeros((E, capacity, D), dtype=xf.dtype).at[routes, pos].set(xf)
        y = jnp.einsum('ecd,efd->ecf', buf, expert_w) + expert_b[:, None, :]
        gathered = y[routes, jnp.minimum(pos, capacity - 1)]
        out = jnp.where(keep[:, None], gathered, xf) * route_probs[:, None]
        return out.reshape(B, S, D)
    h = _L0_tok_ref(x, L0_tok_W0, L0_tok_b0, L0_tok_W1, L0_tok_b1, L0_tok_W2, L0_tok_b2, L0_tok_pos)
    h = h + _L0_attn_ref(_layernorm(h, axis=-1), L0_attn_context_embed, L0_attn_Wq, L0_attn_bq, L0_attn_Wk, L0_attn_bk, L0_attn_Wv, L0_attn_bv, L0_attn_Wo, L0_attn_bo)
    h = h + _L0_ffn_ref(_layernorm(h, axis=-1), L0_ffn_switch_w, L0_ffn_switch_b, L0_ffn_expert_w, L0_ffn_expert_b)
    return h

_drawn_inputs = setup_inputs


def setup_inputs(seed=0):
    import zlib

    import numpy as np

    out = dict(_drawn_inputs(seed))
    spreads = {'L0_ffn_switch_b': (0.0, 0.655), 'L0_ffn_expert_b': (0.0, 2.0)}
    factors = {'L0_tok_b0': 8.0,
     'L0_tok_b1': 8.0,
     'L0_tok_b2': 8.0,
     'L0_attn_context_embed': 5.567,
     'L0_attn_Wq': 5.624,
     'L0_attn_bq': 8.0,
     'L0_attn_Wk': 5.655,
     'L0_attn_bk': 64.0,
     'L0_attn_Wv': 4.141,
     'L0_ffn_expert_w': 22.822,
     'L0_attn_bv': 8.0,
     'L0_attn_bo': 7.688,
     'L0_ffn_switch_w': 4.568}
    for name, (base, spread) in spreads.items():
        noise = np.random.default_rng([zlib.crc32(name.encode()), seed]).standard_normal(out[name].shape)
        drawn = base * np.exp(spread * noise) if base else spread * noise
        out[name] = jnp.asarray(drawn.astype(out[name].dtype))
    for name, factor in factors.items():
        out[name] = (out[name] * factor).astype(out[name].dtype)
    return out
```

```python
from contextlib import ExitStack

import concourse.bass as bass
from concourse import mybir

BATCH, SEQ, CH = 64, 250, 64
D = 128
TAPS = (4, 8, 16)
LEN = SEQ - max(TAPS) + 1
SLOTS = LEN + 1
TILE = SLOTS // 2
NT = 4
GROUPS = BATCH // 2
COLS = NT * TILE
GTOK = 2 * LEN
PAIRS = max(TAPS) // 2
CTX = 1024
NC = CTX // 128
SCALE = float(D) ** -0.5
EPS = 1e-5
E = 16
NTOK = BATCH * LEN
CAP = int(1.2 * NTOK / E)
ET = -(-CAP // 128)
REGION = ET * 128
ROW = 272
XN0, H20, PR, TOK = 0, 128, 256, 257
FAR = 1.0e6
VW = 2 * D + 2
UNROLL = 4
LAST_LAG = 4
PEELED = 7
RING = 4


class Tau:

    def __init__(self, i, c):
        self.i, self.c = i, c

    def at(self, lag, k=1, off=0):
        const = k * (self.c - lag) + off
        return const if self.i is None else self.i * (UNROLL * k) + const

    def halves(self, lag, k, off=0):
        const = k * ((self.c - lag) // 2) + off
        return const if self.i is None else self.i * (UNROLL // 2 * k) + const

    def slot(self, lag, n):
        return (self.c - lag) % n

    def has(self, lag):
        return self.i is not None or 0 <= self.c - lag < GROUPS

    def peeled(self):
        return self.i is None


def wait(eng, sem, value):
    if isinstance(value, int) and value <= 0:
        return
    eng.wait_ge(sem, value)


def pipeline(eng, step):
    for c in range(PEELED):
        step(Tau(None, c))
    with eng.Fori(0, (GROUPS - 1 - PEELED) // UNROLL) as i:
        for c in range(PEELED, PEELED + UNROLL):
            step(Tau(i, c))
    for c in range(GROUPS - 1, GROUPS + LAST_LAG):
        step(Tau(None, c))


def expert_pairs(eng, body):
    body(0)
    with eng.Fori(1, E // 2) as i:
        body(i)


class Chain:

    def __init__(self, eng, sem, per_group):
        self.eng, self.sem, self.n, self.base, self.k = eng, sem, per_group, 0, 0

    def begin(self, tau, lag):
        self.base, self.k = tau.at(lag, self.n), 0

    def add(self, ins):
        ins.then_inc(self.sem, 1)
        self.k += 1

    def sync(self, back=0):
        self.eng.wait_ge(self.sem, self.base + (self.k - back))

    def end(self):
        assert self.k == self.n, (self.k, self.n)


def build(nc, x, w0, b0, w1, b1, w2, b2, pos, ctxe, wq, bq, wk, bk, wv, bv, wo, bo, sw, sbias, ew, eb, out):
    dt = mybir.dt
    f32, f32r, bf16, i32 = dt.float32, dt.float32r, dt.bfloat16, dt.int32
    ALU = mybir.AluOpType
    ACT = mybir.ActivationFunctionType
    X = mybir.AxisListType.X
    slots_dram = nc.dram_tensor("slots", (E * REGION, ROW), f32, kind="Internal").ap()
    out_rows = out.rearrange("b l d -> (b l) d")

    ctx = ExitStack()
    with ctx:
        def on(stack):
            return lambda name, shape, t=f32: stack.enter_context(nc.sbuf_tensor(name, shape, t))

        def sem(name):
            return ctx.enter_context(nc.semaphore(name))

        sb = on(ctx)
        ident = sb("ident", [128, 128])
        ident_b = sb("ident_b", [128, 128], bf16)
        tri = sb("tri", [TILE, TILE], bf16)
        ones_b = sb("ones_b", [TILE, TILE], bf16)
        code = sb("code", [TILE, NT, E])
        code_m = sb("code_m", [TILE, NT, E])
        no_token = sb("no_token", [TILE, NT])
        token_of = sb("token_of", [TILE, NT])
        minus_half = sb("minus_half", [TILE, NT])
        conv_hi = sb("conv_hi", [128, PAIRS * D], f32r)
        conv_lo = sb("conv_lo", [128, PAIRS * D], f32r)
        posb = sb("posb", [TILE, 2, D])
        key_max = sb("key_max", [128, CTX], f32r)
        key_hi = sb("key_hi", [128, CTX], f32r)
        key_lo = sb("key_lo", [128, CTX], f32r)
        key_bias = sb("key_bias", [128, NC])
        val = sb("val", [128, NC * VW], f32r)
        sw_parts = sb("sw_parts", [128, 2 * E], f32r)
        sbias_bc = sb("sbias_bc", [TILE, E])
        ew_hi = sb("ew_hi", [128, E * D], f32r)
        ew_lo = sb("ew_lo", [128, E * D], f32r)
        eb_bc = sb("eb_bc", [128, E * D])
        x_in = [sb(f"x_in{k}", [128, 2, 2, 128]) for k in range(2)]
        x_hi = sb("x_hi", [128, 2, SEQ], f32r)
        x_lo = sb("x_lo", [128, 2, SEQ], f32r)
        hT = sb("hT", [128, COLS])
        h = [sb(f"h{k}", [TILE, NT, D]) for k in range(4)]
        stats1 = sb("stats1", [TILE, NT, 6])
        stats2 = sb("stats2", [TILE, NT, 6])
        tmp1 = sb("tmp1", [TILE, 8, NT])
        tmp2 = sb("tmp2", [TILE, 8, NT])
        xn = sb("xn", [TILE, NT, D])
        xnT_hi = [sb(f"xnT_hi{k}", [128, COLS], f32r) for k in range(2)]
        xnT_lo = [sb(f"xnT_lo{k}", [128, COLS], f32r) for k in range(2)]
        half_max = sb("half_max", [TILE, NT, 2])
        row_max = sb("row_max", [TILE, NT])
        max_hi = sb("max_hi", [TILE, NT], bf16)
        max_lo = sb("max_lo", [TILE, NT], bf16)
        rden = sb("rden", [TILE, NT])
        part = sb("part", [TILE, NT, D])
        row = [sb(f"row{k}", [TILE, NT, ROW]) for k in range(2)]
        x2T_hi = sb("x2T_hi", [128, COLS], f32r)
        x2T_lo = sb("x2T_lo", [128, COLS], f32r)
        logit = sb("logit", [TILE, NT, E])
        rel = sb("rel", [TILE, NT, E])
        erel = sb("erel", [TILE, NT, E])
        pick = sb("pick", [TILE, NT, E])
        best = sb("best", [TILE, NT])
        hot = sb("hot", [TILE, NT + 1, E], bf16)
        count = sb("count", [TILE, NT, E])
        base = sb("base", [TILE, E])
        rt = sb("rt", [TILE, 6, NT])
        slot_i = [sb(f"slot_i{k}", [TILE, NT], i32) for k in range(2)]
        out_b = [sb(f"out_b{k}", [TILE, NT, D]) for k in range(2)]

        with ExitStack() as s1:
            st = on(s1)
            w_raw = st("w_raw", [D, max(TAPS) * CH])
            w_raw1 = st("w_raw1", [D, TAPS[1] * CH])
            w_raw0 = st("w_raw0", [D, TAPS[0] * CH])
            b_raw = st("b_raw", [TILE, 3, D])
            wq_s, wk_s, wv_s, wo_s = (st(n, [D, D]) for n in ("wq_s", "wk_s", "wv_s", "wo_s"))
            bcols = st("bcols", [D, 3])
            bo_bc = st("bo_bc", [128, D])
            ctx_s = st("ctx_s", [128, NC, D])
            ctxT = st("ctxT", [128, CTX])
            kT = st("kT", [128, CTX])
            vT = st("vT", [128, CTX])
            wq2 = st("wq2", [128, D])
            wqT = st("wqT", [128, D])
            val_f = st("val_f", [128, NC, D])
            sw_s = st("sw_s", [E, D])
            ew_s = st("ew_s", [D, E, D])
            blank = st("blank", [128, 3, ROW])
        with ExitStack() as s2:
            st = on(s2)
            p_hi = [st(f"p_hi{k}", [128, NC, COLS], f32r) for k in range(2)]
            p_lo = [st(f"p_lo{k}", [128, NC, COLS], f32r) for k in range(2)]
            p_f = [st(f"p_f{k}", [128, COLS]) for k in range(RING)]
        with ExitStack() as s3:
            st = on(s3)
            ex = [st(f"ex{k}", [128, ET, ROW]) for k in range(2)]
            exT_hi = st("exT_hi", [128, REGION], f32r)
            exT_lo = st("exT_lo", [128, REGION], f32r)
            ey = st("ey", [128, ET, D])
            eout = [st(f"eout{k}", [128, ET, D]) for k in range(2)]
            etok = [st(f"etok{k}", [128, ET], i32) for k in range(2)]

        bank = [ctx.enter_context(nc.psum_tensor(f"bank{k}", [128, 512], f32)) for k in range(8)]
        WA, WB, MAXB, SCB, PVB = bank[0], bank[1], bank[2:4], bank[4:6], bank[6:8]
        XNB, XTB = MAXB

        ld_conv, ld_pos, ld_attn, ld_moe, blanked = (sem(n) for n in ("ld_conv", "ld_pos", "ld_attn", "ld_moe", "blanked"))
        consts, su_pe, su_ev = sem("consts"), sem("su_pe"), sem("su_ev")
        ld_x = [sem(f"ld_x{k}") for k in range(2)]
        xT_ready, xhi_ready, xlo_ready = sem("xT_ready"), sem("xhi_ready"), sem("xlo_ready")
        conv_ready, hT_ready, htok_ready, h_ready = sem("conv_ready"), sem("hT_ready"), sem("htok_ready"), sem("h_ready")
        var1_ready, rstd1_ready, shift1_ready, xn_ready = sem("var1_ready"), sem("rstd1_ready"), sem("shift1_ready"), sem("xn_ready")
        xnT_ready, xnhi_ready, xnlo_ready = sem("xnT_ready"), sem("xnhi_ready"), sem("xnlo_ready")
        half_ready, half_read, max_ready, maxrow_ready, shiftrow_ready = (sem(n) for n in ("half_ready", "half_read", "max_ready", "maxrow_ready", "shiftrow_ready"))
        score_ready, exp_ready, plo_ready = sem("score_ready"), sem("exp_ready"), sem("plo_ready")
        pv_ready, h2_ready = sem("pv_ready"), sem("h2_ready")
        var2_ready, rstd2_ready, shift2_ready, x2_ready = sem("var2_ready"), sem("rstd2_ready"), sem("shift2_ready"), sem("x2_ready")
        x2T_ready, x2hi_ready, x2lo_ready = sem("x2T_ready"), sem("x2hi_ready"), sem("x2lo_ready")
        logits_ready, logits_read, rel_ready, erel_ready = sem("logits_ready"), sem("logits_read"), sem("rel_ready"), sem("erel_ready")
        hot_ready, count_ready, count_read, row_ready = sem("hot_ready"), sem("count_ready"), sem("count_read"), sem("row_ready")
        out_ready = sem("out_ready")
        scattered = [sem(f"scattered{k}") for k in range(2)]
        stored = [sem(f"stored{k}") for k in range(2)]
        c_ln1, c_ln2, c_max, c_pv, c_rt1, c_rt2, c_out = (sem(n) for n in ("c_ln1", "c_ln2", "c_max", "c_pv", "c_rt1", "c_rt2", "c_out"))
        ld_ex = [sem(f"ld_ex{k}") for k in range(2)]
        exT_ready, exhi_ready, exlo_ready, ey_ready, ey_read, eout_ready, etok_ready = (sem(n) for n in ("exT_ready", "exhi_ready", "exlo_ready", "ey_ready", "ey_read", "eout_ready", "etok_ready"))
        ex_free = sem("ex_free")
        pool_passed = sem("pool_passed")
        final = [sem(f"final{k}") for k in range(2)]

        block = ctx.enter_context(nc.Block())

        marks = {}

        @block.vector
        def _(dve):
            v = nc.vector
            n_ev = [0]

            def seq(ins, mark=None):
                ins.then_inc(su_ev, 1)
                n_ev[0] += 1
                dve.wait_ge(su_ev, n_ev[0])
                if mark:
                    marks[mark] = n_ev[0]

            def split(hi, lo, src, mark=None):
                seq(v.tensor_copy(hi, src))
                seq(v.tensor_tensor(lo, src, hi.bitcast(f32), ALU.subtract), mark)

            seq(v.memset(posb[:, :, :], 0.0))
            seq(v.memset(x_hi[:, :, SEQ - 1].bitcast(f32), 0.0))
            seq(v.memset(x_lo[:, :, SEQ - 1].bitcast(f32), 0.0))
            seq(v.memset(xn[:, :, 0], 1.0))
            seq(v.memset(row[0][:, :, :], 0.0))
            seq(v.memset(row[1][:, :, :], 0.0))
            seq(v.memset(hot[:, NT, :], 0.0))
            dve.wait_ge(consts, 3)
            seq(v.tensor_copy(ident_b[:, :], ident[:, :]))
            dve.wait_ge(ld_conv, 48)
            n1, n0 = TAPS[1] * CH, TAPS[0] * CH
            seq(v.tensor_tensor(w_raw[:, 0:n1], w_raw[:, 0:n1], w_raw1[:, :], ALU.add))
            seq(v.tensor_tensor(w_raw[:, 0:n0], w_raw[:, 0:n0], w_raw0[:, :], ALU.add))
            seq(v.tensor_scalar(w_raw[:, :], w_raw[:, :], 1.0 / 3, None, ALU.mult), "taps")
            dve.wait_ge(su_pe, 1)
            for half in range(2):
                cols = slice(half * 512, (half + 1) * 512)
                split(conv_hi[:, cols], conv_lo[:, cols], bank[half][:, :], "conv")
            dve.wait_ge(ld_pos, 80)
            seq(v.tensor_tensor(b_raw[:, 0, :], b_raw[:, 0, :], b_raw[:, 1, :], ALU.add))
            seq(v.tensor_tensor(b_raw[:, 0, :], b_raw[:, 0, :], b_raw[:, 2, :], ALU.add))
            for t in range(2):
                seq(v.scalar_tensor_tensor(posb[:, t, :], b_raw[:, 0, :], 1.0 / 3, posb[:, t, :], ALU.mult, ALU.add))
            dve.wait_ge(ld_attn, 16 * 9)
            dve.wait_ge(su_pe, 2)
            seq(v.tensor_copy(wqT[:, :], bank[2][:, 0:D]))
            seq(v.tensor_scalar(wq2[:, :], wqT[:, :], wqT[:, 0:1], None, ALU.subtract))
            seq(v.tensor_copy(wq2[:, 0:1], bcols[:, 0:1]), "wq2")
            seq(v.tensor_copy(sw_parts[:, 0:E], bank[2][:, D:D + E]))
            seq(v.tensor_tensor(sw_parts[:, E:2 * E], bank[2][:, D:D + E], sw_parts[:, 0:E].bitcast(f32), ALU.subtract), "sw")
            dve.wait_ge(su_pe, 3)
            seq(v.tensor_copy(ctxT[:, 0:512], bank[3][:, :]))
            seq(v.tensor_copy(ctxT[:, 512:1024], bank[4][:, :]), "ctxT")
            dve.wait_ge(su_pe, 4)
            seq(v.tensor_scalar(kT[:, 0:512], bank[5][:, :], bcols[:, 1:2], None, ALU.add))
            seq(v.tensor_scalar(kT[:, 512:1024], bank[6][:, :], bcols[:, 1:2], None, ALU.add), "kT")
            dve.wait_ge(su_pe, 5)
            seq(v.tensor_scalar(vT[:, 0:512], bank[7][:, :], bcols[:, 2:3], None, ALU.add))
            seq(v.tensor_scalar(vT[:, 512:1024], bank[0][:, :], bcols[:, 2:3], None, ALU.add), "vT")
            dve.wait_ge(su_pe, 6)
            for half in range(2):
                cols = slice(half * 512, (half + 1) * 512)
                seq(v.tensor_copy(key_max[:, cols], bank[1 + half][:, :]))
                split(key_hi[:, cols], key_lo[:, cols], bank[1 + half][:, :], "keys")
            seq(v.memset(key_hi[0:1, :].bitcast(f32), 1.0))
            seq(v.memset(key_lo[0:1, :].bitcast(f32), 0.0))
            dve.wait_ge(su_pe, 7)
            seq(v.tensor_scalar(key_bias[:, :], bank[3][:, 0:NC], SCALE, None, ALU.mult), "key_bias")
            dve.wait_ge(su_pe, 8)
            val3 = val[:, :].rearrange("p (j c) -> p j c", c=VW)
            bo4 = bo_bc[:, :].unsqueeze(1).broadcast_to([128, 4, D])
            for half in range(2):
                js = slice(half * 4, half * 4 + 4)
                seq(v.tensor_tensor(val_f[:, js, :], bank[4 + half][:, :].rearrange("p (j c) -> p j c", c=D), bo4, ALU.add), "val_f")
            split(val3[:, :, 0:D], val3[:, :, D + 2:VW], val_f[:, :, :])
            seq(v.memset(val3[:, :, D].bitcast(f32), 1.0))
            seq(v.memset(val3[:, :, D + 1].bitcast(f32), 0.0))
            for q in range(4):
                dve.wait_ge(su_pe, 9 + q)
                cols = slice(q * 512, (q + 1) * 512)
                split(ew_hi[:, cols], ew_lo[:, cols], bank[(6 + q) % 8][:, :], f"ew{q}")
            dve.wait_ge(consts, 10)
            dve.wait_ge(ld_moe, 80)
            seq(v.tensor_scalar(base[:, :], code[:, 0, :], -float(REGION), float(E * REGION - 1), ALU.mult, ALU.add), "setup")

            ln1, ln2 = Chain(dve, c_ln1, 6), Chain(dve, c_ln2, 6)
            mx, pv = Chain(dve, c_max, 2), Chain(dve, c_pv, 2 * NT)
            rt1, rt2 = Chain(dve, c_rt1, 7), Chain(dve, c_rt2, 8)

            def x_low(tau, lag):
                dve.wait_ge(xhi_ready, tau.at(lag, 1, 1))
                cols = (slice(None), slice(None), slice(0, SEQ - 1))
                v.tensor_tensor(x_lo[cols], XTB[:, 0:2 * SEQ].rearrange("p (b s) -> p b s", b=2)[cols],
                                x_hi[cols].bitcast(f32), ALU.subtract).then_inc(xlo_ready, 1)

            def stats(src, st, tmp, chain, ready, tau, lag):
                for t in range(NT):
                    ins = v.bn_stats(st[:, t, :], src[:, t, :])
                chain.add(ins)
                chain.sync()
                chain.add(v.tensor_tensor(tmp[:, 0, :], st[:, :, 1], st[:, :, 4], ALU.add))
                chain.add(v.tensor_tensor(tmp[:, 1, :], st[:, :, 1], st[:, :, 4], ALU.subtract))
                chain.add(v.tensor_tensor(tmp[:, 2, :], st[:, :, 2], st[:, :, 5], ALU.add))
                chain.sync(1)
                chain.add(v.tensor_tensor(tmp[:, 3, :], tmp[:, 1, :], tmp[:, 1, :], ALU.mult))
                chain.sync()
                chain.add(v.scalar_tensor_tensor(tmp[:, 4, :], tmp[:, 2, :], 4.0 / D, tmp[:, 3, :], ALU.mult, ALU.add))
                chain.sync()
                v.tensor_scalar(tmp[:, 5, :], tmp[:, 4, :], 0.25, EPS, ALU.mult, ALU.add).then_inc(ready, 1)
                chain.end()

            def shift(tmp, rstd_ready, done, tau, lag):
                dve.wait_ge(rstd_ready, tau.at(lag, 1, 1))
                v.scalar_tensor_tensor(tmp[:, 7, :], tmp[:, 0, :], -0.5, tmp[:, 6, :], ALU.mult, ALU.mult).then_inc(done, 1)

            def maxima(tau, ks):
                for k in ks:
                    dve.wait_ge(half_ready, tau.at(1, 2 * NT, k + 1))
                    v.reduce_max(half_max[:, k // 2, k % 2:k % 2 + 1], MAXB[k % 2][0:TILE, :], X).then_inc(half_read, 1)

            def max_rows(tau):
                mx.begin(tau, 1)
                dve.wait_ge(half_read, tau.at(1, 2 * NT, 2 * NT))
                mx.add(v.tensor_tensor(row_max[:, :], half_max[:, :, 0], half_max[:, :, 1], ALU.max))
                mx.sync()
                mx.add(v.tensor_copy(max_hi[:, :], row_max[:, :]))
                mx.sync()
                v.tensor_tensor(max_lo[:, :], row_max[:, :], max_hi[:, :], ALU.subtract).then_inc(max_ready, 1)
                mx.end()

            def combine(tau, t):
                k, b = tau.slot(2, 2), PVB[t % 2]
                if t == 0:
                    pv.begin(tau, 2)
                    wait(dve, scattered[k], tau.halves(2, 64))
                dve.wait_ge(pv_ready, tau.at(2, NT, t + 1))
                pv.add(v.reciprocal(rden[:, t:t + 1], b[0:TILE, D:D + 1]))
                pv.sync()
                pv.add(v.scalar_tensor_tensor(part[:, t, :], b[0:TILE, 0:D], rden[:, t:t + 1],
                                              h[tau.slot(2, 4)][:, t, :], ALU.mult, ALU.add))
                pv.sync()
                v.scalar_tensor_tensor(row[k][:, t, H20:H20 + D], b[0:TILE, D + 2:VW], rden[:, t:t + 1],
                                       part[:, t, :], ALU.mult, ALU.add).then_inc(h2_ready, 1)
                if t == NT - 1:
                    pv.end()

            def logits(tau):
                rt1.begin(tau, 3)
                dve.wait_ge(logits_ready, tau.at(3, 1, 1))
                parts = WA[0:TILE, 0:NT * 2 * E].rearrange("p (t c) -> p t c", c=2 * E)
                bias = sbias_bc[:, :].unsqueeze(1).broadcast_to([TILE, NT, E])
                rt1.add(v.tensor_tensor(logit[:, :, :], parts[:, :, 0:E], bias, ALU.add))
                rt1.sync()
                rt1.add(v.tensor_tensor(logit[:, :, :], parts[:, :, E:2 * E], logit[:, :, :], ALU.add))
                rt1.sync()
                rt1.add(v.reduce_max(best[:, :], logit[:, :, :], X))
                rt1.sync()
                v.tensor_tensor(rel[:, :, :], logit[:, :, :], best[:, :].unsqueeze(2).broadcast_to([TILE, NT, E]),
                                ALU.subtract).then_inc(rel_ready, 1)

            def one_hot(tau):
                dve.wait_ge(rel_ready, tau.at(3, 1, 1))
                rt1.add(v.scalar_tensor_tensor(pick[:, :, :], rel[:, :, :], 0.0, code_m[:, :, :], ALU.is_equal, ALU.mult))
                rt1.sync()
                rt1.add(v.reduce_max(rt[:, 0, :], pick[:, :, :], X))
                rt1.sync()
                v.tensor_tensor(hot[:, 0:NT, :], code[:, :, :], rt[:, 0, :].unsqueeze(2).broadcast_to([TILE, NT, E]),
                                ALU.is_equal).then_inc(hot_ready, 1)
                dve.wait_ge(erel_ready, tau.at(3, 1, 1))
                rt1.add(v.reduce_sum(rt[:, 1, :], erel[:, :, :], X))
                rt1.sync()
                rt1.add(v.reciprocal(row[tau.slot(3, 2)][:, :, PR], rt[:, 1, :]))
                rt1.end()

            def slots(tau):
                k = tau.slot(3, 2)
                rt2.begin(tau, 3)
                dve.wait_ge(count_ready, tau.at(3, 1, 1))
                c5 = WA[0:TILE, 0:(NT + 1) * E].rearrange("p (t c) -> p t c", c=E)
                rt2.add(v.tensor_tensor(count[:, :, :], c5[:, 0:NT, :], base[:, :].unsqueeze(1).broadcast_to([TILE, NT, E]), ALU.add))
                rt2.sync()
                v.tensor_tensor(base[:, :], c5[:, NT, :], base[:, :], ALU.add).then_inc(count_read, 1)
                rt2.add(v.tensor_tensor(count[:, :, :], count[:, :, :], hot[:, 0:NT, :], ALU.mult))
                rt2.sync()
                rt2.add(v.reduce_sum(rt[:, 2, :], count[:, :, :], X))
                rt2.sync()
                rt2.add(v.tensor_tensor(rt[:, 3, :], rt[:, 2, :], no_token[:, :], ALU.add))
                rt2.sync()
                rt2.add(v.scalar_tensor_tensor(rt[:, 4, :], rt[:, 0, :], float(REGION), rt[:, 3, :], ALU.mult, ALU.add))
                rt2.sync()
                rt2.add(v.tensor_scalar(rt[:, 5, :], rt[:, 4, :], float(E * REGION + CAP), FAR, ALU.is_ge, ALU.mult))
                rt2.sync()
                rt2.add(v.tensor_tensor(slot_i[k][:, :], rt[:, 5, :], rt[:, 3, :], ALU.add))
                rt2.add(v.tensor_scalar(token_of[:, :], token_of[:, :], float(GTOK), None, ALU.add))
                rt2.sync()
                v.tensor_copy(row[k][:, :, TOK], token_of[:, :]).then_inc(row_ready, 1)
                rt2.end()

            def pass_through(tau):
                k = tau.slot(3, 2)
                wait(dve, stored[k], tau.halves(3, 32))
                dve.wait_ge(x2_ready, tau.at(3, 1, 1))
                for t in range(NT):
                    ins = v.scalar_tensor_tensor(out_b[k][:, t, :], row[k][:, t, XN0:XN0 + D], row[k][:, t, PR:PR + 1],
                                                 row[k][:, t, H20:H20 + D], ALU.mult, ALU.add)
                ins.then_inc(out_ready, 1)

            def step(tau):
                if tau.has(1):
                    maxima(tau, (0, 1))
                if tau.has(3):
                    shift(tmp2, rstd2_ready, shift2_ready, tau, 3)
                if tau.has(1):
                    maxima(tau, range(2, 2 * NT))
                    max_rows(tau)
                if tau.has(2):
                    combine(tau, 0)
                if tau.has(0):
                    ln1.begin(tau, 0)
                    dve.wait_ge(htok_ready, tau.at(0, 1, 1))
                    tiles = WA[0:TILE, :].rearrange("p (b c) -> p b c", b=2)
                    hs = h[tau.slot(0, 4)]
                    pos2 = posb[:, :, :].rearrange("p a c -> p (a c)").unsqueeze(1).broadcast_to([TILE, 2, 2 * D])
                    v.tensor_tensor(hs[:, :, :].rearrange("p (b a) c -> p b (a c)", b=2), tiles, pos2, ALU.add).then_inc(h_ready, 1)
                    dve.wait_ge(h_ready, tau.at(0, 1, 1))
                    stats(hs, stats1, tmp1, ln1, var1_ready, tau, 0)
                if tau.has(2):
                    combine(tau, 1)
                if tau.has(0):
                    shift(tmp1, rstd1_ready, shift1_ready, tau, 0)
                if tau.has(-1):
                    x_low(tau, -1)
                if tau.has(3):
                    dve.wait_ge(x2hi_ready, tau.at(3, 1, 1))
                    v.tensor_tensor(x2T_lo[:, :], WA[:, 0:COLS], x2T_hi[:, :].bitcast(f32), ALU.subtract).then_inc(x2lo_ready, 1)
                if tau.has(2):
                    combine(tau, 2)
                if tau.has(3):
                    logits(tau)
                    one_hot(tau)
                if tau.has(2):
                    combine(tau, 3)
                if tau.has(0):
                    dve.wait_ge(xnhi_ready, tau.at(0, 1, 1))
                    k = tau.slot(0, 2)
                    v.tensor_tensor(xnT_lo[k][:, :], XNB[:, 0:COLS], xnT_hi[k][:, :].bitcast(f32), ALU.subtract).then_inc(xnlo_ready, 1)
                if tau.has(3):
                    slots(tau)
                    pass_through(tau)
                if tau.has(2):
                    ln2.begin(tau, 2)
                    dve.wait_ge(h2_ready, tau.at(2, NT, NT))
                    stats(row[tau.slot(2, 2)][:, :, H20:H20 + D], stats2, tmp2, ln2, var2_ready, tau, 2)

            x_low(Tau(None, 0), 0)
            pipeline(dve, step)

            def expert_finish(i):
                for k in range(2):
                    e = i * 2 + k
                    dve.wait_ge(ld_ex[k], i * 16 + 16)
                    wait(dve, final[k], i * (16 * ET))
                    v.tensor_copy(etok[k][:, :], ex[k][:, :, TOK]).then_inc(etok_ready, 1)
                    for q in range(3):
                        cols = slice(q * 384, (q + 1) * 384)
                        dve.wait_ge(exhi_ready, i * 6 + (k * 3 + q + 1))
                        v.tensor_tensor(exT_lo[:, cols], bank[q][:, 0:384], exT_hi[:, cols].bitcast(f32),
                                        ALU.subtract).then_inc(exlo_ready, 1)
                    for q in range(3):
                        dve.wait_ge(ey_ready, i * 6 + (k * 3 + q + 1))
                        bias = eb_bc[:, bass.ds(e * D, D)].unsqueeze(1).broadcast_to([128, 3, D])
                        v.tensor_tensor(ey[:, q * 3:q * 3 + 3, :], bank[3 + q][:, 0:384].rearrange("p (t c) -> p t c", c=D),
                                        bias, ALU.add).then_inc(ey_read, 1)
                        dve.wait_ge(ey_read, i * 6 + (k * 3 + q + 1))
                        for t in range(q * 3, q * 3 + 3):
                            ins = v.scalar_tensor_tensor(eout[k][:, t, :], ey[:, t, :], ex[k][:, t, PR:PR + 1],
                                                         ex[k][:, t, H20:H20 + D], ALU.mult, ALU.add)
                            ins.then_inc(eout_ready, 1)
                    dve.wait_ge(eout_ready, i * (2 * ET) + (k + 1) * ET)
                    v.tensor_copy(rden[:, 0:1], rden[:, 0:1]).then_inc(ex_free, 1)

            expert_pairs(dve, expert_finish)

        @block.sync
        def _(sp):
            def load_x(g_tau, lag):
                k = g_tau.slot(lag, 2)
                wait(sp, xT_ready, g_tau.at(lag, 1, -1))
                o = g_tau.at(lag, 2 * SEQ * CH)
                a = bass.AP(x.tensor, o, [[CH, 128], [SEQ * CH, 2], [1, 2 * CH]])
                b = bass.AP(x.tensor, o + 128 * CH, [[CH, SEQ - 129], [SEQ * CH, 2], [1, 2 * CH]])
                sp.dma_start(x_in[k][:, :, 0, :], a).then_inc(ld_x[k], 16)
                sp.dma_start(x_in[k][0:SEQ - 129, :, 1, :], b).then_inc(ld_x[k], 16)

            sp.dma_start(w_raw[:, :], w2).then_inc(ld_conv, 16)
            sp.dma_start(w_raw1[:, :], w1).then_inc(ld_conv, 16)
            sp.dma_start(w_raw0[:, :], w0).then_inc(ld_conv, 16)
            load_x(Tau(None, 0), 0)
            sp.dma_start(ctx_s[:, :, :], ctxe.rearrange("(j p) d -> p j d", p=128)).then_inc(ld_attn, 16)
            for t, w in ((wq_s, wq), (wk_s, wk), (wv_s, wv), (wo_s, wo)):
                sp.dma_start(t[:, :], w).then_inc(ld_attn, 16)
            load_x(Tau(None, 1), 0)
            for half in range(2):
                es = slice(half * E // 2, (half + 1) * E // 2)
                sp.dma_start(ew_s[:, es, :], ew[es, :, :].rearrange("e f d -> f e d")).then_inc(ld_moe, 16)
            sp.dma_start(eb_bc[:, :], bass.AP(eb.tensor, 0, [[0, 128], [1, E * D]])).then_inc(ld_moe, 16)
            sp.wait_ge(consts, 3)
            for r in range(E * REGION // (128 * 3)):
                rows = slots_dram[r * 384:(r + 1) * 384, :].rearrange("(p a) c -> p a c", p=128)
                sp.dma_start(rows, blank[:, :, :]).then_inc(blanked, 16)

            def step(tau):
                if tau.has(-1) and (tau.i is not None or tau.c > 0):
                    load_x(tau, -1)
                if tau.has(3):
                    k = tau.slot(3, 2)
                    sp.wait_ge(out_ready, tau.at(3, 1, 1))
                    o = tau.at(3, GTOK * D)
                    for half, n in ((0, TILE), (1, TILE - 1)):
                        rows = bass.AP(out.tensor, o + half * TILE * D, [[D, n], [LEN * D, 2], [1, D]])
                        sp.dma_start(rows, out_b[k][0:n, half::2, :]).then_inc(stored[k], 16)

            pipeline(sp, step)

            for k in range(2):
                sp.wait_ge(scattered[k], 64 * GROUPS // 2)

            def load_expert(e, k, first):
                if not first:
                    sp.wait_ge(ex_free, e - 1)
                rows = bass.AP(slots_dram.tensor, e * (REGION * ROW), [[ROW, 128], [128 * ROW, ET], [1, ROW]])
                sp.dma_start(ex[k][:, :, :], rows).then_inc(ld_ex[k], 16)

            load_expert(0, 0, True)
            load_expert(1, 1, True)
            with sp.Fori(1, E // 2) as i:
                for k in range(2):
                    load_expert(i * 2 + k, k, False)

        @block.gpsimd
        def _(pool):
            g = nc.gpsimd
            g.memset(ident[:, :], 0.0).then_inc(c_out, 1)
            g.memset(tri[:, :], 1.0).then_inc(c_out, 1)
            g.memset(blank[:, :, :], 0.0).then_inc(c_out, 1)
            pool.wait_ge(c_out, 3)
            g.affine_select(out=ident[:, :], in_=ident[:, :], compare_op=ALU.not_equal, fill=1.0, base=0,
                            pattern=[[-1, 128]], channel_multiplier=1).then_inc(consts, 1)
            g.affine_select(out=tri[:, :], in_=tri[:, :], compare_op=ALU.is_ge, fill=0.0, base=0,
                            pattern=[[1, TILE]], channel_multiplier=-1).then_inc(consts, 1)
            g.memset(blank[:, :, TOK], FAR).then_inc(consts, 1)
            g.memset(ones_b[:, :], 1.0).then_inc(consts, 1)
            g.memset(minus_half[:, :], -0.5).then_inc(consts, 1)
            g.iota(code[:, :, :], [[0, NT], [-1, E]], base=E, channel_multiplier=0,
                   allow_small_or_imprecise_dtypes=True).then_inc(consts, 1)
            g.iota(token_of[:, :], [[LEN, 2], [TILE, 2]], base=-GTOK, channel_multiplier=1,
                   allow_small_or_imprecise_dtypes=True).then_inc(consts, 1)
            g.memset(no_token[:, :], 0.0).then_inc(consts, 1)
            pool.wait_ge(consts, 8)
            g.affine_select(out=no_token[:, :], in_=no_token[:, :], compare_op=ALU.is_gt, fill=FAR, base=TILE,
                            pattern=[[0, 2], [-1, 2]], channel_multiplier=-1).then_inc(consts, 1)
            g.affine_select(out=code_m[:, :, :], in_=code[:, :, :], compare_op=ALU.is_gt, fill=0.0, base=TILE,
                            pattern=[[0, 2], [-1, 2], [0, E]], channel_multiplier=-1).then_inc(consts, 1)
            pool.wait_ge(consts, 10)
            pool.wait_ge(blanked, 16 * (E * REGION // 384))

            def rstd(ready, tmp, done, tau, lag):
                pool.wait_ge(ready, tau.at(lag, 1, 1))
                g.tensor_tensor(tmp[:, 6, :], tmp[:, 5, :], minus_half[:, :], ALU.pow).then_inc(done, 1)

            def low_part(tau, j):
                pool.wait_ge(exp_ready, tau.at(1, NC, j + 1))
                k = tau.slot(1, 2)
                g.tensor_tensor(p_lo[k][:, j, :], p_f[j % RING][:, :], p_hi[k][:, j, :].bitcast(f32),
                                ALU.subtract).then_inc(plo_ready, 1)

            def scatter(tau, t):
                k = tau.slot(4, 2)
                pool.wait_ge(row_ready, tau.at(4, 1, 1))
                pool.sem_inc(pool_passed, 1)
                pool.indirect_dma_start(slots_dram[:, :], bass.IndirectOffsetOnAxis(ap=slot_i[k][:, t:t + 1], axis=0),
                                        row[k][:, t, :], None, bounds_check=E * REGION - 1,
                                        oob_is_err=False).then_inc(scattered[k], 16)

            def step(tau):
                if tau.has(4):
                    for t in range(NT):
                        scatter(tau, t)
                if tau.has(0):
                    rstd(var1_ready, tmp1, rstd1_ready, tau, 0)
                if tau.has(1):
                    for j in range(NC):
                        low_part(tau, j)
                if tau.has(2):
                    rstd(var2_ready, tmp2, rstd2_ready, tau, 2)

            pipeline(pool, step)

            for k in range(2):
                pool.wait_ge(stored[k], 32 * GROUPS // 2)
            def expert_scatter(i):
                for k in range(2):
                    pool.wait_ge(etok_ready, i * 2 + (k + 1))
                    pool.sem_inc(pool_passed, 1)
                    for t in range(ET):
                        pool.wait_ge(eout_ready, i * (2 * ET) + (k * ET + t + 1))
                        pool.sem_inc(pool_passed, 1)
                        pool.indirect_dma_start(out_rows, bass.IndirectOffsetOnAxis(ap=etok[k][:, t:t + 1], axis=0),
                                                eout[k][:, t, :], None, bounds_check=NTOK - 1,
                                                oob_is_err=False).then_inc(final[k], 16)

            expert_pairs(pool, expert_scatter)
            for k in range(2):
                pool.wait_ge(final[k], 16 * ET * (E // 2))

        @block.scalar
        def _(act):
            a = nc.scalar
            for k, (b, n) in enumerate(((b0, 0), (b1, 1), (b2, 2))):
                act.dma_start(b_raw[:, n, :], bass.AP(b.tensor, 0, [[0, TILE], [1, D]])).then_inc(ld_pos, 16)
            act.wait_ge(su_ev, 1)
            act.dma_start(posb[:, 0, :], pos[0, 0:TILE, :]).then_inc(ld_pos, 16)
            act.dma_start(posb[0:LEN - TILE, 1, :], pos[0, TILE:LEN, :]).then_inc(ld_pos, 16)
            for n, b in enumerate((bq, bk, bv)):
                act.dma_start(bcols[:, n:n + 1], b.rearrange("(p a) -> p a", a=1)).then_inc(ld_attn, 16)
            act.dma_start(bo_bc[:, :], bass.AP(bo.tensor, 0, [[0, 128], [1, D]])).then_inc(ld_attn, 16)
            act.dma_start(sw_s[:, :], sw).then_inc(ld_moe, 16)
            act.dma_start(sbias_bc[:, :], bass.AP(sbias.tensor, 0, [[0, TILE], [1, E]])).then_inc(ld_moe, 16)

            def x_high(tau, lag):
                act.wait_ge(xT_ready, tau.at(lag, 1, 1))
                a.activation(x_hi[:, :, 0:SEQ - 1], XTB[:, 0:2 * SEQ].rearrange("p (b s) -> p b s", b=2)[:, :, 0:SEQ - 1],
                             ACT.Copy).then_inc(xhi_ready, 1)

            def exps(tau, j):
                k = tau.slot(1, 2)
                act.wait_ge(score_ready, tau.at(1, NC, j + 1))
                wait(act, plo_ready, tau.at(1, NC, j + 1 - RING))
                if j == 0:
                    wait(act, pv_ready, tau.at(3, NT, NT))
                s = SCB[j % 2][:, 0:COLS]
                a.activation(p_f[j % RING][:, :], s, ACT.Exp, bias=key_bias[:, j:j + 1], scale=SCALE)
                a.activation(p_hi[k][:, j, :], s, ACT.Exp, bias=key_bias[:, j:j + 1], scale=SCALE).then_inc(exp_ready, 1)

            def normalise(ready, src, tmp, dst, first, done, tau, lag):
                act.wait_ge(ready, tau.at(lag, 1, 1))
                for t in range(NT):
                    ins = a.activation(dst[:, t, first:D], src[:, t, first:D], ACT.Identity,
                                       bias=tmp[:, 7, t:t + 1], scale=tmp[:, 6, t:t + 1])
                ins.then_inc(done, 1)

            def step(tau):
                if tau.has(3):
                    normalise(shift2_ready, row[tau.slot(3, 2)][:, :, H20:H20 + D], tmp2, row[tau.slot(3, 2)], 0,
                              x2_ready, tau, 3)
                if tau.has(0):
                    act.wait_ge(conv_ready, tau.at(0, 1, 1))
                    a.activation(hT[:, :], WB[:, 0:COLS], ACT.Copy).then_inc(hT_ready, 1)
                if tau.has(1):
                    act.wait_ge(maxrow_ready, tau.at(1, 1, 1))
                    a.activation(xnT_hi[tau.slot(1, 2)][0:1, :], WB[0:1, 0:COLS], ACT.Copy,
                                 scale=-1.0).then_inc(shiftrow_ready, 1)
                if tau.has(-1):
                    x_high(tau, -1)
                if tau.has(1):
                    exps(tau, 0)
                if tau.has(3):
                    act.wait_ge(x2T_ready, tau.at(3, 1, 1))
                    a.activation(x2T_hi[:, :], WA[:, 0:COLS], ACT.Copy).then_inc(x2hi_ready, 1)
                if tau.has(1):
                    exps(tau, 1)
                if tau.has(0):
                    normalise(shift1_ready, h[tau.slot(0, 4)], tmp1, xn, 1, xn_ready, tau, 0)
                if tau.has(1):
                    exps(tau, 2)
                    exps(tau, 3)
                if tau.has(3):
                    act.wait_ge(rel_ready, tau.at(3, 1, 1))
                    a.activation(erel[:, :, :], rel[:, :, :], ACT.Exp).then_inc(erel_ready, 1)
                if tau.has(0):
                    act.wait_ge(xnT_ready, tau.at(0, 1, 1))
                    a.activation(xnT_hi[tau.slot(0, 2)][:, :], XNB[:, 0:COLS], ACT.Copy).then_inc(xnhi_ready, 1)
                if tau.has(1):
                    exps(tau, 4)
                    exps(tau, 5)
                    exps(tau, 6)
                    exps(tau, 7)

            act.wait_ge(su_ev, marks["setup"])
            x_high(Tau(None, 0), 0)
            pipeline(act, step)

            def expert_high(i):
                for n in range(6):
                    q = n % 3
                    act.wait_ge(exT_ready, i * 6 + (n + 1))
                    if q == 0:
                        wait(act, ey_ready, i * 6 + n)
                    a.activation(exT_hi[:, q * 384:(q + 1) * 384], bank[q][:, 0:384], ACT.Copy).then_inc(exhi_ready, 1)

            expert_pairs(act, expert_high)

        @block.tensor
        def _(pe):
            m, tp = nc.tensor.matmul, nc.tensor.transpose

            pe.wait_ge(consts, 3)
            pe.wait_ge(su_ev, marks["taps"])
            for j in range(PAIRS):
                ins = tp(bank[j // 4][:, (j % 4) * 128:(j % 4 + 1) * 128], w_raw[:, j * 128:(j + 1) * 128], ident[:, :])
            ins.then_inc(su_pe, 1)
            pe.wait_ge(ld_attn, 16 * 9)
            pe.wait_ge(ld_moe, 80)
            tp(bank[2][:, 0:D], wq_s[:, :], ident[:, :])
            tp(bank[2][:, D:D + E], sw_s[:, :], ident[0:E, 0:E]).then_inc(su_pe, 1)
            for j in range(NC):
                ins = tp(bank[3 + j // 4][:, (j % 4) * 128:(j % 4 + 1) * 128], ctx_s[:, j, :], ident[:, :])
            ins.then_inc(su_pe, 1)
            pe.wait_ge(su_ev, marks["ctxT"])
            for half in range(2):
                ins = m(bank[5 + half][:, :], wk_s[:, :], ctxT[:, half * 512:(half + 1) * 512], start=True, stop=True)
            ins.then_inc(su_pe, 1)
            for half in range(2):
                ins = m(bank[(7 + half) % 8][:, :], wv_s[:, :], ctxT[:, half * 512:(half + 1) * 512], start=True, stop=True)
            ins.then_inc(su_pe, 1)
            pe.wait_ge(su_ev, marks["kT"])
            for half in range(2):
                ins = m(bank[1 + half][:, :], wq2[:, :], kT[:, half * 512:(half + 1) * 512], start=True, stop=True)
            ins.then_inc(su_pe, 1)
            for j in range(NC):
                ins = m(bank[3][:, j:j + 1], kT[:, j * 128:(j + 1) * 128], bcols[:, 0:1], start=True, stop=True)
            ins.then_inc(su_pe, 1)
            pe.wait_ge(su_ev, marks["vT"])
            for j in range(NC):
                ins = m(bank[4 + j // 4][:, (j % 4) * 128:(j % 4 + 1) * 128], vT[:, j * 128:(j + 1) * 128], wo_s[:, :],
                        start=True, stop=True)
            ins.then_inc(su_pe, 1)
            pe.wait_ge(su_ev, marks["keys"])
            for q in range(4):
                for n in range(4):
                    ins = tp(bank[(6 + q) % 8][:, n * 128:(n + 1) * 128], ew_s[:, q * 4 + n, :], ident[:, :])
                ins.then_inc(su_pe, 1)

            def x_transposed(tau, lag):
                k = tau.slot(lag, 2)
                pe.wait_ge(ld_x[k], tau.halves(lag, 32, 32))
                for b in range(2):
                    tp(XTB[:, b * SEQ:b * SEQ + 128], x_in[k][:, b, 0, :], ident[:, :])
                    ins = tp(XTB[:, b * SEQ + 128:b * SEQ + SEQ - 1], x_in[k][0:SEQ - 129, b, 1, :],
                             ident[0:SEQ - 129, 0:SEQ - 129])
                ins.then_inc(xT_ready, 1)

            def conv(pairs):
                for j in pairs:
                    for w, xx in ((conv_hi, x_hi), (conv_hi, x_lo), (conv_lo, x_hi)):
                        ins = m(WB[:, 0:COLS], w[:, j * D:(j + 1) * D], xx[:, :, 2 * j:2 * j + SLOTS],
                                start=(j == 0 and w is conv_hi and xx is x_hi), stop=(j == PAIRS - 1 and w is conv_lo))
                return ins

            def tiles_transposed(src, dst, n):
                for t in range(NT):
                    ins = tp(dst(t), src(t), ident[0:n, 0:n])
                return ins

            def max_pass(tau, ks):
                q = tau.slot(1, 2)
                if ks[0] == 0:
                    pe.wait_ge(xnhi_ready, tau.at(1, 1, 1))
                    pe.wait_ge(xnlo_ready, tau.at(1, 1, 1))
                for k in ks:
                    wait(pe, half_read, tau.at(1, 2 * NT, k - 1))
                    t, c = k // 2, k % 2
                    m(MAXB[c][0:TILE, :], xnT_hi[q][:, t * TILE:(t + 1) * TILE], key_max[:, c * 512:(c + 1) * 512],
                      start=True, stop=True).then_inc(half_ready, 1)

            def score(tau, j):
                q = tau.slot(1, 2)
                wait(pe, exp_ready, tau.at(1, NC, j - 1))
                if j == 0:
                    pe.wait_ge(shiftrow_ready, tau.at(1, 1, 1))
                    pe.wait_ge(xnlo_ready, tau.at(1, 1, 1))
                b, ks = SCB[j % 2][:, 0:COLS], slice(j * 128, (j + 1) * 128)
                m(b, key_hi[:, ks], xnT_hi[q][:, :], start=True, stop=False)
                m(b, key_hi[:, ks], xnT_lo[q][:, :], start=False, stop=False)
                m(b, key_lo[:, ks], xnT_hi[q][:, :], start=False, stop=True).then_inc(score_ready, 1)

            def p_times_v(tau, t, js):
                q, b = tau.slot(2, 2), PVB[t % 2]
                if js[0] == 0:
                    wait(pe, h2_ready, tau.at(2, NT, t - 1))
                    if t == 0:
                        pe.wait_ge(exp_ready, tau.at(2, NC, NC))
                        pe.wait_ge(plo_ready, tau.at(2, NC, NC))
                for j in js:
                    cols = slice(t * TILE, (t + 1) * TILE)
                    m(b[0:TILE, 0:VW], p_hi[q][:, j, cols], val[:, j * VW:(j + 1) * VW], start=(j == 0), stop=False)
                    ins = m(b[0:TILE, 0:D + 2], p_lo[q][:, j, cols], val[:, j * VW:j * VW + D + 2], start=False, stop=(j == NC - 1))
                if js[-1] == NC - 1:
                    ins.then_inc(pv_ready, 1)

            def max_row(tau):
                pe.wait_ge(max_ready, tau.at(1, 1, 1))
                if tau.has(0):
                    pe.wait_ge(hT_ready, tau.at(0, 1, 1))
                else:
                    pe.wait_ge(shiftrow_ready, tau.at(1))
                for t in range(NT):
                    o = WB[0:1, t * TILE:(t + 1) * TILE]
                    m(o, max_hi[:, t:t + 1], ident_b[0:TILE, 0:TILE], start=True, stop=False)
                    ins = m(o, max_lo[:, t:t + 1], ident_b[0:TILE, 0:TILE], start=False, stop=True)
                ins.then_inc(maxrow_ready, 1)

            def x2_transposed(tau):
                pe.wait_ge(x2_ready, tau.at(3, 1, 1))
                if tau.has(0):
                    pe.wait_ge(h_ready, tau.at(0, 1, 1))
                else:
                    pe.wait_ge(count_read, tau.at(3))
                r = row[tau.slot(3, 2)]
                tiles_transposed(lambda t: r[:, t, XN0:XN0 + D], lambda t: WA[:, t * TILE:(t + 1) * TILE],
                                 TILE).then_inc(x2T_ready, 1)

            def logits(tau):
                pe.wait_ge(x2hi_ready, tau.at(3, 1, 1))
                pe.wait_ge(x2lo_ready, tau.at(3, 1, 1))
                for t in range(NT):
                    cols = slice(t * TILE, (t + 1) * TILE)
                    m(WA[0:TILE, t * 2 * E:(t + 1) * 2 * E], x2T_hi[:, cols], sw_parts[:, :], start=True, stop=False)
                    ins = m(WA[0:TILE, t * 2 * E:t * 2 * E + E], x2T_lo[:, cols], sw_parts[:, 0:E], start=False, stop=True)
                ins.then_inc(logits_ready, 1)

            def counts(tau):
                pe.wait_ge(hot_ready, tau.at(3, 1, 1))
                pe.wait_ge(consts, 10)
                pe.wait_ge(rel_ready, tau.at(3, 1, 1))
                flat = hot[:, :, :].rearrange("p t c -> p (t c)")
                m(WA[0:TILE, 0:(NT + 1) * E], tri[:, :], flat, start=True, stop=False)
                for n in range(1, NT + 1):
                    ins = m(WA[0:TILE, n * E:(NT + 1) * E], ones_b[:, :], flat[:, 0:(NT + 1 - n) * E], start=False, stop=(n == NT))
                ins.then_inc(count_ready, 1)

            def conv_quarter(tau, q):
                if tau.has(0):
                    if q == 0:
                        pe.wait_ge(xhi_ready, tau.at(0, 1, 1))
                        pe.wait_ge(xlo_ready, tau.at(0, 1, 1))
                        wait(pe, shiftrow_ready, tau.at(1))
                    ins = conv(range(q * PAIRS // 4, (q + 1) * PAIRS // 4))
                    if q == 3:
                        ins.then_inc(conv_ready, 1)

            def step(tau):
                first, second = range(NC // 2), range(NC // 2, NC)

                def maxes(ks):
                    if tau.has(1):
                        max_pass(tau, ks)

                def pv(t, js):
                    if tau.has(2):
                        p_times_v(tau, t, js)

                def scores(j):
                    if tau.has(1):
                        score(tau, j)

                conv_quarter(tau, 0)
                conv_quarter(tau, 1)
                maxes((0, 1))
                conv_quarter(tau, 2)
                maxes((2, 3))
                conv_quarter(tau, 3)
                maxes((4, 5))
                pv(0, first)
                maxes((6, 7))
                pv(0, second)
                if tau.has(0):
                    pe.wait_ge(hT_ready, tau.at(0, 1, 1))
                    wait(pe, count_read, tau.at(4, 1, 1))
                    tiles_transposed(lambda t: hT[:, t * TILE:(t + 1) * TILE], lambda t: WA[0:TILE, t * D:(t + 1) * D],
                                     128).then_inc(htok_ready, 1)
                pv(1, first)
                if tau.has(1):
                    max_row(tau)
                if tau.has(-1):
                    if not tau.has(1):
                        wait(pe, xlo_ready, tau.at(0, 1, 1))
                    x_transposed(tau, -1)
                pv(1, second)
                scores(0)
                if tau.has(3):
                    x2_transposed(tau)
                pv(2, first)
                scores(1)
                pv(2, second)
                scores(2)
                if tau.has(3):
                    logits(tau)
                pv(3, first)
                scores(3)
                if tau.has(0):
                    pe.wait_ge(xn_ready, tau.at(0, 1, 1))
                    tiles_transposed(lambda t: xn[:, t, :], lambda t: XNB[:, t * TILE:(t + 1) * TILE],
                                     TILE).then_inc(xnT_ready, 1)
                scores(4)
                pv(3, second)
                scores(5)
                if tau.has(3):
                    counts(tau)
                scores(6)
                scores(7)

            pe.wait_ge(su_ev, marks["setup"])
            x_transposed(Tau(None, 0), 0)
            pipeline(pe, step)

            def expert_products(i):
                for k in range(2):
                    pe.wait_ge(ld_ex[k], i * 16 + 16)
                    wait(pe, exlo_ready, i * 6 + k * 3)
                    for q in range(3):
                        for t in range(3):
                            ins = tp(bank[q][:, t * 128:(t + 1) * 128], ex[k][:, q * 3 + t, XN0:XN0 + D], ident[:, :])
                        ins.then_inc(exT_ready, 1)
                    wait(pe, ey_read, i * 6 + k * 3)
                    for q in range(3):
                        pe.wait_ge(exlo_ready, i * 6 + (k * 3 + q + 1))
                        for t in range(3):
                            rows = slice((q * 3 + t) * 128, (q * 3 + t + 1) * 128)
                            o = bank[3 + q][:, t * 128:(t + 1) * 128]
                            w = bass.ds(i * (2 * D) + k * D, D)
                            m(o, exT_hi[:, rows], ew_hi[:, w], start=True, stop=False)
                            m(o, exT_lo[:, rows], ew_hi[:, w], start=False, stop=False)
                            ins = m(o, exT_hi[:, rows], ew_lo[:, w], start=False, stop=True)
                        ins.then_inc(ey_ready, 1)

            expert_pairs(pe, expert_products)


_INS = ["x", "L0_tok_W0", "L0_tok_b0", "L0_tok_W1", "L0_tok_b1", "L0_tok_W2", "L0_tok_b2", "L0_tok_pos",
        "L0_attn_context_embed", "L0_attn_Wq", "L0_attn_bq", "L0_attn_Wk", "L0_attn_bk", "L0_attn_Wv", "L0_attn_bv",
        "L0_attn_Wo", "L0_attn_bo", "L0_ffn_switch_w", "L0_ffn_switch_b", "L0_ffn_expert_w", "L0_ffn_expert_b"]


def kernel(**inputs):
    import numpy as np
    import concourse.bacc as bacc
    from concourse.bass_utils import run_bass_kernel_spmd

    nc = bacc.Bacc("TRN2", target_bir_lowering=False, num_devices=1)
    arrays, args = {}, []
    for name in _INS:
        a = np.ascontiguousarray(inputs[name])
        arrays[f"in_{name}"] = a
        args.append(nc.dram_tensor(f"in_{name}", a.shape, mybir.dt.from_np(a.dtype), kind="ExternalInput").ap())
    args.append(nc.dram_tensor("out", (BATCH, LEN, D), mybir.dt.float32, kind="ExternalOutput").ap())
    build(nc, *args)
    return run_bass_kernel_spmd(nc, [arrays], core_ids=[0]).results[0]["out"]
```

```python
from contextlib import ExitStack

import concourse.bass as bass
from concourse import mybir

BATCH, SEQ, CH = 64, 250, 64
D = 128
TAPS = (4, 8, 16)
LEN = SEQ - max(TAPS) + 1
SLOTS = LEN + 1
TILE = SLOTS // 2
NT = 4
GROUPS = BATCH // 2
COLS = NT * TILE
GTOK = 2 * LEN
PAIRS = max(TAPS) // 2
CTX = 1024
NC = CTX // 128
SCALE = float(D) ** -0.5
EPS = 1e-5
E = 16
NTOK = BATCH * LEN
CAP = int(1.2 * NTOK / E)
ET = -(-CAP // 128)
REGION = ET * 128
ROW = 272
XN0, H20, PR, TOK = 0, 128, 256, 257
FAR = 1.0e6
VW = 2 * D + 2
UNROLL = 4
LAST_LAG = 4
PEELED = 7
EARLY = NC - 2
ROWS = 4
RING = 4


class Tau:

    def __init__(self, i, c):
        self.i, self.c = i, c

    def at(self, lag, k=1, off=0):
        const = k * (self.c - lag) + off
        return const if self.i is None else self.i * (UNROLL * k) + const

    def halves(self, lag, k, off=0):
        const = k * ((self.c - lag) // 2) + off
        return const if self.i is None else self.i * (UNROLL // 2 * k) + const

    def rings(self, lag, k):
        const = k * ((self.c - lag) // ROWS)
        return const if self.i is None else self.i * (UNROLL // ROWS * k) + const

    def slot(self, lag, n):
        return (self.c - lag) % n

    def has(self, lag):
        return self.i is not None or 0 <= self.c - lag < GROUPS

    def first(self):
        return self.i is None and self.c == 0

    def second(self):
        return self.i is None and self.c == 1


def wait(eng, sem, value):
    if isinstance(value, int) and value <= 0:
        return
    eng.wait_ge(sem, value)


def pipeline(eng, step, before=None):
    before = before or {}
    for c in range(PEELED):
        if c in before:
            before[c]()
        step(Tau(None, c))
    with eng.Fori(0, (GROUPS - 1 - PEELED) // UNROLL) as i:
        for c in range(PEELED, PEELED + UNROLL):
            step(Tau(i, c))
    for c in range(GROUPS - 1, GROUPS + LAST_LAG):
        if c in before:
            before[c]()
        step(Tau(None, c))


def expert_pairs(eng, body):
    body(0)
    with eng.Fori(1, E // 2) as i:
        body(i)


class Chain:

    def __init__(self, eng, sem, per_group):
        self.eng, self.sem, self.n, self.base, self.k = eng, sem, per_group, 0, 0

    def begin(self, tau, lag):
        self.base, self.k = tau.at(lag, self.n), 0

    def add(self, ins):
        ins.then_inc(self.sem, 1)
        self.k += 1

    def sync(self, back=0):
        self.eng.wait_ge(self.sem, self.base + (self.k - back))

    def end(self):
        assert self.k == self.n, (self.k, self.n)


def build(nc, x, w0, b0, w1, b1, w2, b2, pos, ctxe, wq, bq, wk, bk, wv, bv, wo, bo, sw, sbias, ew, eb, out):
    dt = mybir.dt
    f32, f32r, bf16, i32 = dt.float32, dt.float32r, dt.bfloat16, dt.int32
    ALU = mybir.AluOpType
    ACT = mybir.ActivationFunctionType
    X = mybir.AxisListType.X
    slots_dram = nc.dram_tensor("slots", (E * REGION, ROW), f32, kind="Internal").ap()
    out_rows = out.rearrange("b l d -> (b l) d")

    ctx = ExitStack()
    with ctx:
        def on(stack):
            return lambda name, shape, t=f32: stack.enter_context(nc.sbuf_tensor(name, shape, t))

        def sem(name):
            return ctx.enter_context(nc.semaphore(name))

        sb = on(ctx)
        ident = sb("ident", [128, 128])
        ident_b = sb("ident_b", [128, 128], bf16)
        tri = sb("tri", [TILE, TILE], bf16)
        ones_b = sb("ones_b", [TILE, TILE], bf16)
        code = sb("code", [TILE, NT, E])
        code_m = sb("code_m", [TILE, NT, E])
        no_token = sb("no_token", [TILE, NT])
        token_of = sb("token_of", [TILE, NT])
        minus_half = sb("minus_half", [TILE, NT])
        conv_hi = sb("conv_hi", [128, PAIRS * D], f32r)
        conv_lo = sb("conv_lo", [128, PAIRS * D], f32r)
        posb = sb("posb", [TILE, 2, D])
        key_max = sb("key_max", [128, CTX], f32r)
        key_hi = sb("key_hi", [128, CTX], f32r)
        key_lo = sb("key_lo", [128, CTX], f32r)
        key_bias = sb("key_bias", [128, NC])
        val = sb("val", [128, NC * VW], f32r)
        swT = sb("swT", [128, E])
        sbias_bc = sb("sbias_bc", [TILE, E])
        ew_hi = sb("ew_hi", [128, E * D], f32r)
        ew_lo = sb("ew_lo", [128, E * D], f32r)
        eb_bc = sb("eb_bc", [128, E * D])
        ew_s = sb("ew_s", [D, E, D])
        blank = sb("blank", [128, ROW])
        x_in = [sb(f"x_in{k}", [128, 2, 2, 128]) for k in range(2)]
        x_hi = sb("x_hi", [128, 2, SEQ], f32r)
        x_lo = sb("x_lo", [128, 2, SEQ], f32r)
        hT = sb("hT", [128, COLS])
        h = [sb(f"h{k}", [TILE, NT, D]) for k in range(4)]
        stats1 = sb("stats1", [TILE, NT, 6])
        stats2 = sb("stats2", [TILE, NT, 6])
        tmp1 = sb("tmp1", [TILE, 8, NT])
        tmp2 = sb("tmp2", [TILE, 8, NT])
        xn = sb("xn", [TILE, NT, D])
        xnT_hi = [sb(f"xnT_hi{k}", [128, COLS], f32r) for k in range(2)]
        xnT_lo = [sb(f"xnT_lo{k}", [128, COLS], f32r) for k in range(2)]
        half_max = sb("half_max", [TILE, NT, 2])
        row_max = sb("row_max", [TILE, NT])
        max_hi = sb("max_hi", [TILE, NT], bf16)
        max_lo = sb("max_lo", [TILE, NT], bf16)
        rden = sb("rden", [TILE, NT])
        part = sb("part", [TILE, NT, D])
        row = [sb(f"row{k}", [TILE, NT, ROW]) for k in range(ROWS)]
        x2T = sb("x2T", [128, COLS])
        mix = [sb(f"mix{k}", [TILE, 2, NT]) for k in range(ROWS)]
        logit = sb("logit", [TILE, NT, E])
        rel = sb("rel", [TILE, NT, E])
        erel = sb("erel", [TILE, NT, E])
        pick = sb("pick", [TILE, NT, E])
        best = sb("best", [TILE, NT])
        hot = sb("hot", [TILE, NT + 1, E], bf16)
        count = sb("count", [TILE, NT, E])
        base = sb("base", [TILE, E])
        rt = sb("rt", [TILE, 6, NT])
        slot_i = [sb(f"slot_i{k}", [TILE, NT], i32) for k in range(ROWS)]
        out_b = [sb(f"out_b{k}", [TILE, NT, D]) for k in range(2)]

        with ExitStack() as s1:
            st = on(s1)
            w_raw = st("w_raw", [D, max(TAPS) * CH])
            w_raw1 = st("w_raw1", [D, TAPS[1] * CH])
            w_raw0 = st("w_raw0", [D, TAPS[0] * CH])
            b_raw = st("b_raw", [TILE, 3, D])
            wq_s, wk_s, wv_s, wo_s = (st(n, [D, D]) for n in ("wq_s", "wk_s", "wv_s", "wo_s"))
            bcols = st("bcols", [D, 3])
            bo_bc = st("bo_bc", [128, D])
            ctx_s = st("ctx_s", [128, NC, D])
            ctxT = st("ctxT", [128, CTX])
            kT = st("kT", [128, CTX])
            vT = st("vT", [128, CTX])
            wq2 = st("wq2", [128, D])
            wqT = st("wqT", [128, D])
            val_f = st("val_f", [128, NC, D])
            sw_s = st("sw_s", [E, D])
        with ExitStack() as s2:
            st = on(s2)
            p_hi = [st(f"p_hi{k}", [128, NC, COLS], f32r) for k in range(2)]
            p_lo = [st(f"p_lo{k}", [128, NC, COLS], f32r) for k in range(2)]
            p_f = [st(f"p_f{k}", [128, COLS]) for k in range(RING)]
        with ExitStack() as s3:
            st = on(s3)
            ex = [st(f"ex{k}", [128, ET, ROW]) for k in range(2)]
            exT_hi = st("exT_hi", [128, REGION], f32r)
            exT_lo = st("exT_lo", [128, REGION], f32r)
            ey = st("ey", [128, ET, D])
            eout = [st(f"eout{k}", [128, ET, D]) for k in range(2)]
            etok = [st(f"etok{k}", [128, ET], i32) for k in range(2)]

        bank = [ctx.enter_context(nc.psum_tensor(f"bank{k}", [128, 512], f32)) for k in range(8)]
        WA, WB, MAXB, SCB, PVB = bank[0], bank[1], bank[2:4], bank[4:6], bank[6:8]
        XNB, XTB = MAXB

        ld_w2, ld_conv, ld_pos, ld_ctx, ld_attn, ld_bias, ld_moe, blanked = (
            sem(n) for n in ("ld_w2", "ld_conv", "ld_pos", "ld_ctx", "ld_attn", "ld_bias", "ld_moe", "blanked"))
        consts, su_pe, su_ev, su_act = sem("consts"), sem("su_pe"), sem("su_ev"), sem("su_act")
        ewT_ready, ewhi_ready, ewlo_ready = sem("ewT_ready"), sem("ewhi_ready"), sem("ewlo_ready")
        ld_x = [sem(f"ld_x{k}") for k in range(2)]
        xT_ready, xhi_ready, xlo_ready = sem("xT_ready"), sem("xhi_ready"), sem("xlo_ready")
        conv_ready, hT_ready, htok_ready, h_ready = sem("conv_ready"), sem("hT_ready"), sem("htok_ready"), sem("h_ready")
        var1_ready, rstd1_ready, shift1_ready, xn_ready = sem("var1_ready"), sem("rstd1_ready"), sem("shift1_ready"), sem("xn_ready")
        xnT_ready, xnhi_ready, xnlo_ready = sem("xnT_ready"), sem("xnhi_ready"), sem("xnlo_ready")
        half_ready, half_read, max_ready, maxrow_ready, shiftrow_ready = (sem(n) for n in ("half_ready", "half_read", "max_ready", "maxrow_ready", "shiftrow_ready"))
        score_ready, exp_ready, plo_ready = sem("score_ready"), sem("exp_ready"), sem("plo_ready")
        pv_ready, h2_ready = sem("pv_ready"), sem("h2_ready")
        var2_ready, rstd2_ready, shift2_ready, x2_ready = sem("var2_ready"), sem("rstd2_ready"), sem("shift2_ready"), sem("x2_ready")
        x2T_ready, x2T_copied = sem("x2T_ready"), sem("x2T_copied")
        logits_ready, logits_read, rel_ready, erel_ready = sem("logits_ready"), sem("logits_read"), sem("rel_ready"), sem("erel_ready")
        hot_ready, count_ready, count_read, row_ready = sem("hot_ready"), sem("count_ready"), sem("count_read"), sem("row_ready")
        mix_ready, out_ready = sem("mix_ready"), sem("out_ready")
        scattered = [sem(f"scattered{k}") for k in range(ROWS)]
        stored = [sem(f"stored{k}") for k in range(2)]
        c_ln1, c_ln2, c_max, c_pv, c_rt1, c_rt2, c_out = (sem(n) for n in ("c_ln1", "c_ln2", "c_max", "c_pv", "c_rt1", "c_rt2", "c_out"))
        ld_ex = [[sem(f"ld_ex{k}_{q}") for q in range(3)] for k in range(2)]
        exT_ready, exhi_ready, exlo_ready, ey_ready, ey_read, eout_ready, etok_ready = (sem(n) for n in ("exT_ready", "exhi_ready", "exlo_ready", "ey_ready", "ey_read", "eout_ready", "etok_ready"))
        ex_free = sem("ex_free")
        pool_passed = sem("pool_passed")
        final = [sem(f"final{k}") for k in range(2)]

        block = ctx.enter_context(nc.Block())

        marks = {}

        @block.vector
        def _(dve):
            v = nc.vector
            n_ev = [0]

            def seq(ins, mark=None):
                ins.then_inc(su_ev, 1)
                n_ev[0] += 1
                dve.wait_ge(su_ev, n_ev[0])
                if mark:
                    marks[mark] = n_ev[0]

            seq(v.memset(posb[:, :, :], 0.0))
            seq(v.memset(x_hi[:, :, SEQ - 1].bitcast(f32), 0.0))
            seq(v.memset(x_lo[:, :, SEQ - 1].bitcast(f32), 0.0))
            seq(v.memset(xn[:, :, 0], 1.0))
            for k in range(ROWS):
                seq(v.memset(row[k][:, :, TOK:ROW], 0.0))
            seq(v.memset(hot[:, NT, :], 0.0))
            dve.wait_ge(consts, 3)
            seq(v.tensor_copy(ident_b[:, :], ident[:, :]))
            dve.wait_ge(ld_w2, 16)
            dve.wait_ge(ld_conv, 32)
            n1, n0 = TAPS[1] * CH, TAPS[0] * CH
            seq(v.tensor_tensor(w_raw[:, 0:n1], w_raw[:, 0:n1], w_raw1[:, :], ALU.add))
            seq(v.tensor_tensor(w_raw[:, 0:n0], w_raw[:, 0:n0], w_raw0[:, :], ALU.add), "taps")
            for n, half in enumerate((1, 0)):
                cols = slice(half * 512, (half + 1) * 512)
                dve.wait_ge(su_act, n + 1)
                seq(v.scalar_tensor_tensor(conv_lo[:, cols], bank[half][:, :], 1.0 / 3, conv_hi[:, cols].bitcast(f32),
                                           ALU.mult, ALU.subtract), "conv")
            def positions():
                dve.wait_ge(ld_pos, 80)
                seq(v.tensor_tensor(b_raw[:, 0, :], b_raw[:, 0, :], b_raw[:, 1, :], ALU.add))
                seq(v.tensor_tensor(b_raw[:, 0, :], b_raw[:, 0, :], b_raw[:, 2, :], ALU.add))
                for t in range(2):
                    seq(v.scalar_tensor_tensor(posb[:, t, :], b_raw[:, 0, :], 1.0 / 3, posb[:, t, :], ALU.mult, ALU.add))

            def setup_keys():
                dve.wait_ge(su_pe, 3)
                seq(v.tensor_copy(ctxT[:, 0:512], bank[4][:, :]), "ctxT")
                seq(v.tensor_copy(wqT[:, :], bank[2][:, 0:D]))
                seq(v.tensor_scalar(wq2[:, :], wqT[:, :], wqT[:, 0:1], None, ALU.subtract))
                dve.wait_ge(ld_attn, 96)
                seq(v.tensor_copy(wq2[:, 0:1], bcols[:, 0:1]), "wq2")
                dve.wait_ge(su_pe, 4)
                seq(v.tensor_scalar(kT[:, 0:512], bank[6][:, :], bcols[:, 1:2], None, ALU.add), "kT")
                positions()
                seq(v.tensor_copy(swT[:, :], bank[2][:, D:D + E]), "sw")
                dve.wait_ge(su_pe, 5)
                for half in range(2):
                    cols = slice(half * 512, (half + 1) * 512)
                    dve.wait_ge(su_act, 5 + half)
                    seq(v.tensor_tensor(key_lo[:, cols], bank[4 + half][:, :], key_max[:, cols].bitcast(f32), ALU.subtract), "keys")
                seq(v.tensor_copy(key_hi[:, :], key_max[:, :].bitcast(f32)))
                seq(v.memset(key_hi[0:1, :].bitcast(f32), 1.0))
                seq(v.memset(key_lo[0:1, :].bitcast(f32), 0.0))
                dve.wait_ge(su_pe, 6)
                seq(v.tensor_scalar(key_bias[:, :], bank[2][:, D + E:D + E + NC], SCALE, None, ALU.mult), "key_bias")
                dve.wait_ge(su_pe, 7)
                seq(v.tensor_scalar(vT[:, 0:512], bank[6][:, :], bcols[:, 2:3], None, ALU.add), "vT")

            def setup_values():
                dve.wait_ge(su_pe, 8)
                val3 = val[:, :].rearrange("p (j c) -> p j c", c=VW)
                dve.wait_ge(ld_bias, 32)
                bo4 = bo_bc[:, :].unsqueeze(1).broadcast_to([128, 4, D])
                for half in range(2):
                    js = slice(half * 4, half * 4 + 4)
                    seq(v.tensor_tensor(val_f[:, js, :], bank[4 + half][:, :].rearrange("p (j c) -> p j c", c=D), bo4, ALU.add), "val_f")
                seq(v.tensor_copy(val3[:, :, 0:D], val_f[:, :, :]))

            def setup_values_low():
                val3 = val[:, :].rearrange("p (j c) -> p j c", c=VW)
                seq(v.tensor_tensor(val3[:, :, D + 2:VW], val_f[:, :, :], val3[:, :, 0:D].bitcast(f32), ALU.subtract))
                seq(v.memset(val3[:, :, D].bitcast(f32), 1.0))
                seq(v.memset(val3[:, :, D + 1].bitcast(f32), 0.0))
                dve.wait_ge(consts, 10)
                for k in range(ROWS):
                    seq(v.tensor_scalar(row[k][:, :, TOK], token_of[:, :], float((k - ROWS) * GTOK), None, ALU.add))
                seq(v.tensor_scalar(base[:, :], code[:, 0, :], -float(REGION), float(E * REGION - 1), ALU.mult, ALU.add), "setup")

            def expert_low():
                for q in range(4):
                    cols = slice(q * 512, (q + 1) * 512)
                    dve.wait_ge(ewhi_ready, q + 1)
                    v.tensor_tensor(ew_lo[:, cols], bank[1 + q % 3][:, :], ew_hi[:, cols].bitcast(f32), ALU.subtract).then_inc(ewlo_ready, 1)

            ln1, ln2 = Chain(dve, c_ln1, 6), Chain(dve, c_ln2, 6)
            mx, pv = Chain(dve, c_max, 2), Chain(dve, c_pv, 2 * NT)
            rt1, rt2 = Chain(dve, c_rt1, 8), Chain(dve, c_rt2, 7)

            def x_low(tau, lag):
                dve.wait_ge(xhi_ready, tau.at(lag, 1, 1))
                cols = (slice(None), slice(None), slice(0, SEQ - 1))
                v.tensor_tensor(x_lo[cols], XTB[:, 0:2 * SEQ].rearrange("p (b s) -> p b s", b=2)[cols],
                                x_hi[cols].bitcast(f32), ALU.subtract).then_inc(xlo_ready, 1)

            def stats(src, st, tmp, chain, ready, tau, lag):
                for t in range(NT):
                    ins = v.bn_stats(st[:, t, :], src[:, t, :])
                chain.add(ins)
                chain.sync()
                chain.add(v.tensor_tensor(tmp[:, 0, :], st[:, :, 1], st[:, :, 4], ALU.add))
                chain.add(v.tensor_tensor(tmp[:, 1, :], st[:, :, 1], st[:, :, 4], ALU.subtract))
                chain.add(v.tensor_tensor(tmp[:, 2, :], st[:, :, 2], st[:, :, 5], ALU.add))
                chain.sync(1)
                chain.add(v.tensor_tensor(tmp[:, 3, :], tmp[:, 1, :], tmp[:, 1, :], ALU.mult))
                chain.sync()
                chain.add(v.scalar_tensor_tensor(tmp[:, 4, :], tmp[:, 2, :], 4.0 / D, tmp[:, 3, :], ALU.mult, ALU.add))
                chain.sync()
                v.tensor_scalar(tmp[:, 5, :], tmp[:, 4, :], 0.25, EPS, ALU.mult, ALU.add).then_inc(ready, 1)
                chain.end()

            def shift(tmp, rstd_ready, done, tau, lag):
                dve.wait_ge(rstd_ready, tau.at(lag, 1, 1))
                v.scalar_tensor_tensor(tmp[:, 7, :], tmp[:, 0, :], -0.5, tmp[:, 6, :], ALU.mult, ALU.mult).then_inc(done, 1)

            def maxima(tau, ks):
                for k in ks:
                    dve.wait_ge(half_ready, tau.at(1, 2 * NT, k + 1))
                    v.reduce_max(half_max[:, k // 2, k % 2:k % 2 + 1], MAXB[k % 2][0:TILE, :], X).then_inc(half_read, 1)

            def max_rows(tau):
                mx.begin(tau, 1)
                dve.wait_ge(half_read, tau.at(1, 2 * NT, 2 * NT))
                mx.add(v.tensor_tensor(row_max[:, :], half_max[:, :, 0], half_max[:, :, 1], ALU.max))
                mx.sync()
                mx.add(v.tensor_copy(max_hi[:, :], row_max[:, :]))
                mx.sync()
                v.tensor_tensor(max_lo[:, :], row_max[:, :], max_hi[:, :], ALU.subtract).then_inc(max_ready, 1)
                mx.end()

            def combine(tau, t):
                k, b = tau.slot(2, ROWS), PVB[t % 2]
                if t == 0:
                    pv.begin(tau, 2)
                    wait(dve, scattered[k], tau.rings(2, 64))
                    wait(dve, out_ready, tau.at(2 + ROWS, 1, 1))
                dve.wait_ge(pv_ready, tau.at(2, NT, t + 1))
                pv.add(v.reciprocal(rden[:, t:t + 1], b[0:TILE, D:D + 1]))
                pv.sync()
                pv.add(v.scalar_tensor_tensor(part[:, t, :], b[0:TILE, 0:D], rden[:, t:t + 1],
                                              h[tau.slot(2, 4)][:, t, :], ALU.mult, ALU.add))
                pv.sync()
                v.scalar_tensor_tensor(row[k][:, t, H20:H20 + D], b[0:TILE, D + 2:VW], rden[:, t:t + 1],
                                       part[:, t, :], ALU.mult, ALU.add).then_inc(h2_ready, 1)
                if t == NT - 1:
                    pv.end()

            def logits(tau):
                rt1.begin(tau, 3)
                dve.wait_ge(logits_ready, tau.at(3, 1, 1))
                sums = WA[0:TILE, 0:NT * E].rearrange("p (t c) -> p t c", c=E)
                bias = sbias_bc[:, :].unsqueeze(1).broadcast_to([TILE, NT, E])
                rt1.add(v.tensor_tensor(logit[:, :, :], sums, bias, ALU.add))
                rt1.sync()
                rt1.add(v.reduce_max(best[:, :], logit[:, :, :], X))
                rt1.sync()
                v.tensor_tensor(rel[:, :, :], logit[:, :, :], best[:, :].unsqueeze(2).broadcast_to([TILE, NT, E]),
                                ALU.subtract).then_inc(rel_ready, 1)

            def one_hot(tau):
                dve.wait_ge(rel_ready, tau.at(3, 1, 1))
                rt1.add(v.scalar_tensor_tensor(pick[:, :, :], rel[:, :, :], 0.0, code_m[:, :, :], ALU.is_equal, ALU.mult))
                rt1.sync()
                rt1.add(v.reduce_max(rt[:, 0, :], pick[:, :, :], X))
                rt1.sync()
                v.tensor_tensor(hot[:, 0:NT, :], code[:, :, :], rt[:, 0, :].unsqueeze(2).broadcast_to([TILE, NT, E]),
                                ALU.is_equal).then_inc(hot_ready, 1)

            def probability(tau):
                dve.wait_ge(erel_ready, tau.at(3, 1, 1))
                rt1.add(v.reduce_sum(rt[:, 1, :], erel[:, :, :], X))
                rt1.sync()
                rt1.add(v.reciprocal(row[tau.slot(3, ROWS)][:, :, PR], rt[:, 1, :]))

            def slots_and_stats2(tau):
                a, b = tau.has(3), tau.has(2)
                k, st, tmp, src = tau.slot(3, ROWS), stats2, tmp2, row[tau.slot(2, ROWS)]
                if b:
                    ln2.begin(tau, 2)
                    dve.wait_ge(h2_ready, tau.at(2, NT, NT))
                    ln2.add(v.bn_stats(st[:, NT - 1, :], src[:, NT - 1, H20:H20 + D]))
                if a:
                    rt1.sync()
                    rt1.add(v.tensor_tensor(mix[k][:, 0, :], tmp[:, 6, :], row[k][:, :, PR], ALU.mult))
                    rt1.add(v.tensor_tensor(mix[k][:, 1, :], tmp[:, 7, :], row[k][:, :, PR], ALU.mult))
                    rt2.begin(tau, 3)
                    dve.wait_ge(count_ready, tau.at(3, 1, 1))
                    c5 = WA[0:TILE, 0:(NT + 1) * E].rearrange("p (t c) -> p t c", c=E)
                    rt2.add(v.tensor_tensor(count[:, :, :], c5[:, 0:NT, :], base[:, :].unsqueeze(1).broadcast_to([TILE, NT, E]), ALU.add))
                if b:
                    ln2.sync()
                    ln2.add(v.tensor_tensor(tmp[:, 0, :], st[:, :, 1], st[:, :, 4], ALU.add))
                    ln2.add(v.tensor_tensor(tmp[:, 1, :], st[:, :, 1], st[:, :, 4], ALU.subtract))
                    ln2.add(v.tensor_tensor(tmp[:, 2, :], st[:, :, 2], st[:, :, 5], ALU.add))
                if a:
                    rt1.sync()
                    v.tensor_scalar(mix[k][:, 0, :], mix[k][:, 0, :], 1.0, None, ALU.add).then_inc(mix_ready, 1)
                    rt1.end()
                    rt2.sync()
                    v.tensor_tensor(base[:, :], c5[:, NT, :], base[:, :], ALU.add).then_inc(count_read, 1)
                    rt2.add(v.tensor_tensor(count[:, :, :], count[:, :, :], hot[:, 0:NT, :], ALU.mult))
                if b:
                    ln2.sync(1)
                    ln2.add(v.tensor_tensor(tmp[:, 3, :], tmp[:, 1, :], tmp[:, 1, :], ALU.mult))
                if a:
                    rt2.sync()
                    rt2.add(v.reduce_sum(rt[:, 2, :], count[:, :, :], X))
                if b:
                    ln2.sync()
                    ln2.add(v.scalar_tensor_tensor(tmp[:, 4, :], tmp[:, 2, :], 4.0 / D, tmp[:, 3, :], ALU.mult, ALU.add))
                if a:
                    rt2.sync()
                    rt2.add(v.tensor_tensor(rt[:, 3, :], rt[:, 2, :], no_token[:, :], ALU.add))
                    rt2.add(v.tensor_scalar(row[k][:, :, TOK], row[k][:, :, TOK], float(ROWS * GTOK), None, ALU.add))
                if b:
                    ln2.sync()
                    v.tensor_scalar(tmp[:, 5, :], tmp[:, 4, :], 0.25, EPS, ALU.mult, ALU.add).then_inc(var2_ready, 1)
                    ln2.end()
                if a:
                    rt2.sync(1)
                    rt2.add(v.scalar_tensor_tensor(rt[:, 4, :], rt[:, 0, :], float(REGION), rt[:, 3, :], ALU.mult, ALU.add))
                    rt2.sync()
                    rt2.add(v.tensor_scalar(rt[:, 5, :], rt[:, 4, :], float(E * REGION + CAP), FAR, ALU.is_ge, ALU.mult))
                    rt2.sync()
                    v.tensor_tensor(slot_i[k][:, :], rt[:, 5, :], rt[:, 3, :], ALU.add).then_inc(row_ready, 1)
                    rt2.end()

            def step(tau):
                if tau.has(1):
                    maxima(tau, range(4))
                if tau.has(3):
                    shift(tmp2, rstd2_ready, shift2_ready, tau, 3)
                if tau.has(1):
                    maxima(tau, range(4, 2 * NT))
                    max_rows(tau)
                if tau.has(2):
                    combine(tau, 0)
                if tau.has(0):
                    ln1.begin(tau, 0)
                    dve.wait_ge(htok_ready, tau.at(0, 1, 1))
                    tiles = WA[0:TILE, :].rearrange("p (b c) -> p b c", b=2)
                    hs = h[tau.slot(0, 4)]
                    pos2 = posb[:, :, :].rearrange("p a c -> p (a c)").unsqueeze(1).broadcast_to([TILE, 2, 2 * D])
                    v.tensor_tensor(hs[:, :, :].rearrange("p (b a) c -> p b (a c)", b=2), tiles, pos2, ALU.add).then_inc(h_ready, 1)
                    dve.wait_ge(h_ready, tau.at(0, 1, 1))
                    stats(hs, stats1, tmp1, ln1, var1_ready, tau, 0)
                if tau.first():
                    shift(tmp1, rstd1_ready, shift1_ready, tau, 0)
                    setup_values()
                if tau.has(2):
                    combine(tau, 1)
                if tau.has(0) and not tau.first():
                    shift(tmp1, rstd1_ready, shift1_ready, tau, 0)
                if tau.has(-1):
                    x_low(tau, -1)
                if tau.has(2):
                    combine(tau, 2)
                    dve.wait_ge(h2_ready, tau.at(2, NT, NT - 1))
                    for t in range(NT - 1):
                        v.bn_stats(stats2[:, t, :], row[tau.slot(2, ROWS)][:, t, H20:H20 + D])
                if tau.has(3):
                    logits(tau)
                    one_hot(tau)
                if tau.has(0):
                    dve.wait_ge(xnhi_ready, tau.at(0, 1, 1))
                    k = tau.slot(0, 2)
                    v.tensor_tensor(xnT_lo[k][:, :], XNB[:, 0:COLS], xnT_hi[k][:, :].bitcast(f32), ALU.subtract).then_inc(xnlo_ready, 1)
                if tau.has(2):
                    combine(tau, 3)
                if tau.has(3):
                    probability(tau)
                slots_and_stats2(tau)

            x_low(Tau(None, 0), 0)
            pipeline(dve, step, {0: setup_keys, 1: setup_values_low, GROUPS + 3: expert_low})

            def expert_finish(i):
                for k in range(2):
                    e = i * 2 + k
                    for q in range(3):
                        cols = slice(q * 384, (q + 1) * 384)
                        dve.wait_ge(exhi_ready, i * 6 + (k * 3 + q + 1))
                        v.tensor_tensor(exT_lo[:, cols], bank[q][:, 0:384], exT_hi[:, cols].bitcast(f32),
                                        ALU.subtract).then_inc(exlo_ready, 1)
                    wait(dve, final[k], i * (16 * ET))
                    for q in range(3):
                        dve.wait_ge(ld_ex[k][q], i * 16 + 16)
                    v.tensor_copy(etok[k][:, :], ex[k][:, :, TOK]).then_inc(etok_ready, 1)
                    for q in range(3):
                        dve.wait_ge(ey_ready, i * 6 + (k * 3 + q + 1))
                        bias = eb_bc[:, bass.ds(e * D, D)].unsqueeze(1).broadcast_to([128, 3, D])
                        v.tensor_tensor(ey[:, q * 3:q * 3 + 3, :], bank[3 + q][:, 0:384].rearrange("p (t c) -> p t c", c=D),
                                        bias, ALU.add).then_inc(ey_read, 1)
                        dve.wait_ge(ey_read, i * 6 + (k * 3 + q + 1))
                        for t in range(q * 3, q * 3 + 3):
                            ins = v.scalar_tensor_tensor(eout[k][:, t, :], ey[:, t, :], ex[k][:, t, PR:PR + 1],
                                                         ex[k][:, t, H20:H20 + D], ALU.mult, ALU.add)
                            ins.then_inc(eout_ready, 1)
                    dve.wait_ge(eout_ready, i * (2 * ET) + (k + 1) * ET)
                    v.tensor_copy(rden[:, 0:1], rden[:, 0:1]).then_inc(ex_free, 1)

            dve.wait_ge(ld_moe, 48)
            expert_pairs(dve, expert_finish)

        @block.sync
        def _(sp):
            def load_x(g_tau, lag):
                k = g_tau.slot(lag, 2)
                wait(sp, xT_ready, g_tau.at(lag, 1, -1))
                o = g_tau.at(lag, 2 * SEQ * CH)
                a = bass.AP(x.tensor, o, [[CH, 128], [SEQ * CH, 2], [1, 2 * CH]])
                b = bass.AP(x.tensor, o + 128 * CH, [[CH, SEQ - 129], [SEQ * CH, 2], [1, 2 * CH]])
                sp.dma_start(x_in[k][:, :, 0, :], a).then_inc(ld_x[k], 16)
                sp.dma_start(x_in[k][0:SEQ - 129, :, 1, :], b).then_inc(ld_x[k], 16)

            sp.dma_start(w_raw[:, :], w2).then_inc(ld_w2, 16)
            sp.dma_start(w_raw1[:, :], w1).then_inc(ld_conv, 16)
            sp.dma_start(w_raw0[:, :], w0).then_inc(ld_conv, 16)
            load_x(Tau(None, 0), 0)
            sp.dma_start(ctx_s[:, :, :], ctxe.rearrange("(j p) d -> p j d", p=128)).then_inc(ld_ctx, 16)
            sp.dma_start(wq_s[:, :], wq).then_inc(ld_ctx, 16)
            for t, w in ((wk_s, wk), (wv_s, wv), (wo_s, wo)):
                sp.dma_start(t[:, :], w).then_inc(ld_attn, 16)
            for n, b in enumerate((b0, b1, b2)):
                sp.dma_start(b_raw[:, n, :], bass.AP(b.tensor, 0, [[0, TILE], [1, D]])).then_inc(ld_pos, 16)
            sp.wait_ge(su_ev, 1)
            sp.dma_start(posb[:, 0, :], pos[0, 0:TILE, :]).then_inc(ld_pos, 16)
            sp.dma_start(posb[0:LEN - TILE, 1, :], pos[0, TILE:LEN, :]).then_inc(ld_pos, 16)
            sp.dma_start(bo_bc[:, :], bass.AP(bo.tensor, 0, [[0, 128], [1, D]])).then_inc(ld_bias, 16)
            sp.dma_start(sbias_bc[:, :], bass.AP(sbias.tensor, 0, [[0, TILE], [1, E]])).then_inc(ld_bias, 16)
            load_x(Tau(None, 1), 0)

            def load_experts():
                for half in range(2):
                    es = slice(half * E // 2, (half + 1) * E // 2)
                    sp.dma_start(ew_s[:, es, :], ew[es, :, :].rearrange("e f d -> f e d")).then_inc(ld_moe, 16)
                sp.dma_start(eb_bc[:, :], bass.AP(eb.tensor, 0, [[0, 128], [1, E * D]])).then_inc(ld_moe, 16)

            def step(tau):
                if tau.has(-1) and (tau.i is not None or tau.c > 0):
                    load_x(tau, -1)
                if tau.has(4):
                    k = tau.slot(4, 2)
                    sp.wait_ge(out_ready, tau.at(4, 1, 1))
                    o = tau.at(4, GTOK * D)
                    for half, n in ((0, TILE), (1, TILE - 1)):
                        rows = bass.AP(out.tensor, o + half * TILE * D, [[D, n], [LEN * D, 2], [1, D]])
                        sp.dma_start(rows, out_b[k][0:n, half::2, :]).then_inc(stored[k], 16)

            pipeline(sp, step, {5: load_experts})

            for k in range(ROWS):
                sp.wait_ge(scattered[k], 64 * GROUPS // ROWS)

            def load_expert(e, k, first):
                if not first:
                    sp.wait_ge(ex_free, e - 1)
                for q in range(3):
                    rows = bass.AP(slots_dram.tensor, e * (REGION * ROW) + q * (ET // 3 * 128 * ROW),
                                   [[ROW, 128], [128 * ROW, ET // 3], [1, ROW]])
                    sp.dma_start(ex[k][:, q * 3:(q + 1) * 3, :], rows).then_inc(ld_ex[k][q], 16)

            load_expert(0, 0, True)
            load_expert(1, 1, True)
            with sp.Fori(1, E // 2) as i:
                for k in range(2):
                    load_expert(i * 2 + k, k, False)

        @block.gpsimd
        def _(pool):
            g = nc.gpsimd
            g.memset(ident[:, :], 0.0).then_inc(c_out, 1)
            g.memset(tri[:, :], 1.0).then_inc(c_out, 1)
            g.memset(blank[:, :], 0.0).then_inc(c_out, 1)
            pool.wait_ge(c_out, 3)
            g.affine_select(out=ident[:, :], in_=ident[:, :], compare_op=ALU.not_equal, fill=1.0, base=0,
                            pattern=[[-1, 128]], channel_multiplier=1).then_inc(consts, 1)
            g.affine_select(out=tri[:, :], in_=tri[:, :], compare_op=ALU.is_ge, fill=0.0, base=0,
                            pattern=[[1, TILE]], channel_multiplier=-1).then_inc(consts, 1)
            g.memset(blank[:, TOK:TOK + 1], FAR).then_inc(consts, 1)
            g.memset(ones_b[:, :], 1.0).then_inc(consts, 1)
            g.memset(minus_half[:, :], -0.5).then_inc(consts, 1)
            g.iota(code[:, :, :], [[0, NT], [-1, E]], base=E, channel_multiplier=0,
                   allow_small_or_imprecise_dtypes=True).then_inc(consts, 1)
            g.iota(token_of[:, :], [[LEN, 2], [TILE, 2]], base=0, channel_multiplier=1,
                   allow_small_or_imprecise_dtypes=True).then_inc(consts, 1)
            g.memset(no_token[:, :], 0.0).then_inc(consts, 1)
            pool.wait_ge(consts, 8)
            g.affine_select(out=no_token[:, :], in_=no_token[:, :], compare_op=ALU.is_gt, fill=FAR, base=TILE,
                            pattern=[[0, 2], [-1, 2]], channel_multiplier=-1).then_inc(consts, 1)
            g.affine_select(out=code_m[:, :, :], in_=code[:, :, :], compare_op=ALU.is_gt, fill=0.0, base=TILE,
                            pattern=[[0, 2], [-1, 2], [0, E]], channel_multiplier=-1).then_inc(consts, 1)
            pool.wait_ge(consts, 10)

            def rstd(ready, tmp, done, tau, lag):
                pool.wait_ge(ready, tau.at(lag, 1, 1))
                g.tensor_tensor(tmp[:, 6, :], tmp[:, 5, :], minus_half[:, :], ALU.pow).then_inc(done, 1)

            def low_part(tau, j, lag=1):
                pool.wait_ge(exp_ready, tau.at(lag, NC, j + 1))
                k = tau.slot(lag, 2)
                g.tensor_tensor(p_lo[k][:, j, :], p_f[j % RING][:, :], p_hi[k][:, j, :].bitcast(f32),
                                ALU.subtract).then_inc(plo_ready, 1)

            def scatter(tau, t):
                k = tau.slot(4, ROWS)
                pool.wait_ge(row_ready, tau.at(4, 1, 1))
                pool.sem_inc(pool_passed, 1)
                pool.indirect_dma_start(slots_dram[:, :], bass.IndirectOffsetOnAxis(ap=slot_i[k][:, t:t + 1], axis=0),
                                        row[k][:, t, :], None, bounds_check=E * REGION - 1,
                                        oob_is_err=False).then_inc(scattered[k], 16)

            def step(tau):
                if tau.has(2):
                    for j in range(EARLY, NC):
                        low_part(tau, j, 2)
                if tau.has(4):
                    for t in range(NT):
                        scatter(tau, t)
                if tau.has(0):
                    rstd(var1_ready, tmp1, rstd1_ready, tau, 0)
                if tau.has(1):
                    for j in range(EARLY):
                        low_part(tau, j)
                if tau.has(2):
                    rstd(var2_ready, tmp2, rstd2_ready, tau, 2)

            pipeline(pool, step, {LAST_LAG: lambda: pool.wait_ge(blanked, 16 * E)})

            for k in range(2):
                pool.wait_ge(stored[k], 32 * GROUPS // 2)
            def expert_scatter(i):
                for k in range(2):
                    pool.wait_ge(etok_ready, i * 2 + (k + 1))
                    pool.sem_inc(pool_passed, 1)
                    for t in range(ET):
                        pool.wait_ge(eout_ready, i * (2 * ET) + (k * ET + t + 1))
                        pool.sem_inc(pool_passed, 1)
                        pool.indirect_dma_start(out_rows, bass.IndirectOffsetOnAxis(ap=etok[k][:, t:t + 1], axis=0),
                                                eout[k][:, t, :], None, bounds_check=NTOK - 1,
                                                oob_is_err=False).then_inc(final[k], 16)

            expert_pairs(pool, expert_scatter)
            for k in range(2):
                pool.wait_ge(final[k], 16 * ET * (E // 2))

        @block.scalar
        def _(act):
            a = nc.scalar
            act.dma_start(sw_s[:, :], sw).then_inc(ld_ctx, 16)
            for n, b in enumerate((bq, bk, bv)):
                act.dma_start(bcols[:, n:n + 1], b.rearrange("(p a) -> p a", a=1)).then_inc(ld_attn, 16)
            for n, half in enumerate((1, 0)):
                act.wait_ge(su_pe, n + 1)
                a.activation(conv_hi[:, half * 512:(half + 1) * 512], bank[half][:, :], ACT.Copy,
                             scale=1.0 / 3).then_inc(su_act, 1)

            def setup_keys():
                act.wait_ge(su_pe, 3)
                a.activation(ctxT[:, 512:1024], bank[5][:, :], ACT.Copy).then_inc(su_act, 1)
                act.wait_ge(ld_attn, 96)
                act.wait_ge(su_pe, 4)
                a.activation(kT[:, 512:1024], bank[7][:, :], ACT.Identity, bias=bcols[:, 1:2]).then_inc(su_act, 1)
                act.wait_ge(su_pe, 5)
                for half in range(2):
                    a.activation(key_max[:, half * 512:(half + 1) * 512], bank[4 + half][:, :], ACT.Copy).then_inc(su_act, 1)
                act.wait_ge(su_pe, 7)
                a.activation(vT[:, 512:1024], bank[7][:, :], ACT.Identity, bias=bcols[:, 2:3]).then_inc(su_act, 1)

            def expert_matrices_high():
                for q in range(4):
                    act.wait_ge(ewT_ready, q + 1)
                    a.activation(ew_hi[:, q * 512:(q + 1) * 512], bank[1 + q % 3][:, :], ACT.Copy).then_inc(ewhi_ready, 1)

            def blank_experts(es):
                act.wait_ge(consts, 3)
                for e in es:
                    rows = slots_dram[e * REGION:(e + 1) * REGION, :].rearrange("(p a) c -> p a c", p=128)
                    act.dma_start(rows, blank[:, :].unsqueeze(1).broadcast_to([128, ET, ROW])).then_inc(blanked, 16)

            def x_high(tau, lag):
                act.wait_ge(xT_ready, tau.at(lag, 1, 1))
                a.activation(x_hi[:, :, 0:SEQ - 1], XTB[:, 0:2 * SEQ].rearrange("p (b s) -> p b s", b=2)[:, :, 0:SEQ - 1],
                             ACT.Copy).then_inc(xhi_ready, 1)

            def exps(tau, j, lag=1):
                k = tau.slot(lag, 2)
                act.wait_ge(score_ready, tau.at(lag, NC, j + 1))
                wait(act, plo_ready, tau.at(lag, NC, j + 1 - RING))
                if j == 0:
                    wait(act, pv_ready, tau.at(lag + 2, NT, NT))
                s = SCB[j % 2][:, 0:COLS]
                a.activation(p_f[j % RING][:, :], s, ACT.Exp, bias=key_bias[:, j:j + 1], scale=SCALE)
                a.activation(p_hi[k][:, j, :], s, ACT.Exp, bias=key_bias[:, j:j + 1], scale=SCALE).then_inc(exp_ready, 1)

            def normalise(ready, src, tmp, dst, first, done, tau, lag, tiles=range(NT)):
                act.wait_ge(ready, tau.at(lag, 1, 1))
                for t in tiles:
                    ins = a.activation(dst[:, t, first:D], src[:, t, first:D], ACT.Identity,
                                       bias=tmp[:, 7, t:t + 1], scale=tmp[:, 6, t:t + 1])
                if tiles[-1] == NT - 1:
                    ins.then_inc(done, 1)

            def pass_through(tau):
                k, r = tau.slot(4, 2), tau.slot(4, ROWS)
                act.wait_ge(mix_ready, tau.at(4, 1, 1))
                wait(act, stored[k], tau.halves(4, 32))
                for t in range(NT):
                    ins = a.activation(out_b[k][:, t, :], row[r][:, t, H20:H20 + D], ACT.Identity,
                                       bias=mix[r][:, 1, t:t + 1], scale=mix[r][:, 0, t:t + 1])
                ins.then_inc(out_ready, 1)

            def step(tau):
                if tau.has(2):
                    for j in range(EARLY, NC):
                        exps(tau, j, 2)
                if tau.has(3):
                    normalise(shift2_ready, row[tau.slot(3, ROWS)][:, :, H20:H20 + D], tmp2, row[tau.slot(3, ROWS)], 0,
                              x2_ready, tau, 3)
                if tau.has(0):
                    act.wait_ge(conv_ready, tau.at(0, 1, 1))
                    a.activation(hT[:, :], WB[:, 0:COLS], ACT.Copy).then_inc(hT_ready, 1)
                if tau.has(4):
                    pass_through(tau)
                if tau.has(1):
                    act.wait_ge(maxrow_ready, tau.at(1, 1, 1))
                    a.activation(xnT_hi[tau.slot(1, 2)][0:1, :], WB[0:1, 0:COLS], ACT.Copy,
                                 scale=-1.0).then_inc(shiftrow_ready, 1)
                if tau.first():
                    normalise(shift1_ready, h[tau.slot(0, 4)], tmp1, xn, 1, xn_ready, tau, 0)
                if tau.has(-1):
                    x_high(tau, -1)
                if tau.has(1):
                    exps(tau, 0)
                if tau.has(3):
                    act.wait_ge(x2T_ready, tau.at(3, 1, 1))
                    a.activation(x2T[:, :], WA[:, 0:COLS], ACT.Copy).then_inc(x2T_copied, 1)
                if tau.has(1):
                    exps(tau, 1)
                if tau.has(0) and not tau.first():
                    normalise(shift1_ready, h[tau.slot(0, 4)], tmp1, xn, 1, xn_ready, tau, 0, range(2))
                if tau.has(1):
                    exps(tau, 2)
                if tau.has(0) and not tau.first():
                    normalise(shift1_ready, h[tau.slot(0, 4)], tmp1, xn, 1, xn_ready, tau, 0, range(2, NT))
                if tau.has(1):
                    exps(tau, 3)
                if tau.has(0):
                    act.wait_ge(xnT_ready, tau.at(0, 1, 1))
                    a.activation(xnT_hi[tau.slot(0, 2)][:, :], XNB[:, 0:COLS], ACT.Copy).then_inc(xnhi_ready, 1)
                if tau.has(1):
                    exps(tau, 4)
                if tau.has(3):
                    act.wait_ge(rel_ready, tau.at(3, 1, 1))
                    a.activation(erel[:, :, :], rel[:, :, :], ACT.Exp).then_inc(erel_ready, 1)
                if tau.has(1):
                    exps(tau, 5)

            x_high(Tau(None, 0), 0)
            third = E // 3

            def before_step_1():
                blank_experts(range(third))
                act.wait_ge(su_ev, marks["setup"])

            pipeline(act, step, {0: setup_keys, 1: before_step_1,
                                 2: lambda: blank_experts(range(third, 2 * third)),
                                 3: lambda: blank_experts(range(2 * third, E)), GROUPS + 3: expert_matrices_high})

            def expert_high(i):
                for n in range(6):
                    q = n % 3
                    act.wait_ge(exT_ready, i * 6 + (n + 1))
                    if q == 0:
                        wait(act, ey_ready, i * 6 + n)
                    a.activation(exT_hi[:, q * 384:(q + 1) * 384], bank[q][:, 0:384], ACT.Copy).then_inc(exhi_ready, 1)

            expert_pairs(act, expert_high)

        @block.tensor
        def _(pe):
            m, tp = nc.tensor.matmul, nc.tensor.transpose

            pe.wait_ge(consts, 3)
            for half in (1, 0):
                if half:
                    pe.wait_ge(ld_w2, 16)
                else:
                    pe.wait_ge(su_ev, marks["taps"])
                for j in range(half * 4, half * 4 + 4):
                    ins = tp(bank[half][:, (j % 4) * 128:(j % 4 + 1) * 128], w_raw[:, j * 128:(j + 1) * 128], ident[:, :])
                ins.then_inc(su_pe, 1)

            def transposed_context():
                pe.wait_ge(ld_ctx, 48)
                tp(bank[2][:, 0:D], wq_s[:, :], ident[:, :])
                tp(bank[2][:, D:D + E], sw_s[:, :], ident[0:E, 0:E])
                for j in range(NC):
                    ins = tp(bank[4 + j // 4][:, (j % 4) * 128:(j % 4 + 1) * 128], ctx_s[:, j, :], ident[:, :])
                ins.then_inc(su_pe, 1)

            def keys():
                pe.wait_ge(ld_attn, 96)
                pe.wait_ge(su_ev, marks["ctxT"])
                pe.wait_ge(su_act, 3)
                for half in range(2):
                    ins = m(bank[6 + half][:, :], wk_s[:, :], ctxT[:, half * 512:(half + 1) * 512], start=True, stop=True)
                ins.then_inc(su_pe, 1)

            def scoring_keys():
                pe.wait_ge(su_ev, marks["kT"])
                pe.wait_ge(su_act, 4)
                for half in range(2):
                    ins = m(bank[4 + half][:, :], wq2[:, :], kT[:, half * 512:(half + 1) * 512], start=True, stop=True)
                ins.then_inc(su_pe, 1)

            def key_biases_and_values():
                pe.wait_ge(su_ev, marks["sw"])
                for j in range(NC):
                    ins = m(bank[2][:, D + E + j:D + E + j + 1], kT[:, j * 128:(j + 1) * 128], bcols[:, 0:1], start=True, stop=True)
                ins.then_inc(su_pe, 1)
                for half in range(2):
                    ins = m(bank[6 + half][:, :], wv_s[:, :], ctxT[:, half * 512:(half + 1) * 512], start=True, stop=True)
                ins.then_inc(su_pe, 1)

            setup_parts = (transposed_context, keys, scoring_keys, key_biases_and_values)

            def setup_values():
                pe.wait_ge(su_ev, marks["key_bias"])
                pe.wait_ge(su_ev, marks["vT"])
                pe.wait_ge(su_act, 7)
                for j in range(NC):
                    ins = m(bank[4 + j // 4][:, (j % 4) * 128:(j % 4 + 1) * 128], vT[:, j * 128:(j + 1) * 128], wo_s[:, :],
                            start=True, stop=True)
                ins.then_inc(su_pe, 1)

            def expert_matrices():
                pe.wait_ge(ld_moe, 48)
                pe.wait_ge(shiftrow_ready, GROUPS)
                for q in range(4):
                    wait(pe, ewlo_ready, q - 2)
                    for n in range(4):
                        ins = tp(bank[1 + q % 3][:, n * 128:(n + 1) * 128], ew_s[:, q * 4 + n, :], ident[:, :])
                    ins.then_inc(ewT_ready, 1)

            def x_transposed(tau, lag):
                k = tau.slot(lag, 2)
                pe.wait_ge(ld_x[k], tau.halves(lag, 32, 32))
                for b in range(2):
                    tp(XTB[:, b * SEQ:b * SEQ + 128], x_in[k][:, b, 0, :], ident[:, :])
                    ins = tp(XTB[:, b * SEQ + 128:b * SEQ + SEQ - 1], x_in[k][0:SEQ - 129, b, 1, :],
                             ident[0:SEQ - 129, 0:SEQ - 129])
                ins.then_inc(xT_ready, 1)

            def tiles_transposed(src, dst, n):
                for t in range(NT):
                    ins = tp(dst(t), src(t), ident[0:n, 0:n])
                return ins

            def max_pass(tau, ks):
                q = tau.slot(1, 2)
                if ks[0] == 0:
                    pe.wait_ge(xnhi_ready, tau.at(1, 1, 1))
                    pe.wait_ge(xnlo_ready, tau.at(1, 1, 1))
                for k in ks:
                    wait(pe, half_read, tau.at(1, 2 * NT, k - 1))
                    t, c = k // 2, k % 2
                    m(MAXB[c][0:TILE, :], xnT_hi[q][:, t * TILE:(t + 1) * TILE], key_max[:, c * 512:(c + 1) * 512],
                      start=True, stop=True).then_inc(half_ready, 1)

            def score(tau, j, lag=1):
                q = tau.slot(lag, 2)
                wait(pe, exp_ready, tau.at(lag, NC, j - 1))
                if j == 0:
                    if tau.second():
                        pe.wait_ge(su_ev, marks["setup"])
                    pe.wait_ge(shiftrow_ready, tau.at(1, 1, 1))
                    pe.wait_ge(xnlo_ready, tau.at(1, 1, 1))
                b, ks = SCB[j % 2][:, 0:COLS], slice(j * 128, (j + 1) * 128)
                m(b, key_hi[:, ks], xnT_hi[q][:, :], start=True, stop=False)
                m(b, key_hi[:, ks], xnT_lo[q][:, :], start=False, stop=False)
                m(b, key_lo[:, ks], xnT_hi[q][:, :], start=False, stop=True).then_inc(score_ready, 1)

            def p_times_v(tau, t, js):
                q, b = tau.slot(2, 2), PVB[t % 2]
                if js[0] == 0:
                    wait(pe, h2_ready, tau.at(2, NT, t - 1))
                for j in js:
                    if t == 0 and j in (0, EARLY):
                        pe.wait_ge(plo_ready, tau.at(2, NC, EARLY if j == 0 else NC))
                    cols = slice(t * TILE, (t + 1) * TILE)
                    m(b[0:TILE, 0:VW], p_hi[q][:, j, cols], val[:, j * VW:(j + 1) * VW], start=(j == 0), stop=False)
                    ins = m(b[0:TILE, 0:D + 2], p_lo[q][:, j, cols], val[:, j * VW:j * VW + D + 2], start=False, stop=(j == NC - 1))
                if js[-1] == NC - 1:
                    ins.then_inc(pv_ready, 1)

            def max_row(tau):
                pe.wait_ge(max_ready, tau.at(1, 1, 1))
                if tau.has(0):
                    pe.wait_ge(hT_ready, tau.at(0, 1, 1))
                else:
                    pe.wait_ge(shiftrow_ready, tau.at(1))
                for t in range(NT):
                    o = WB[0:1, t * TILE:(t + 1) * TILE]
                    m(o, max_hi[:, t:t + 1], ident_b[0:TILE, 0:TILE], start=True, stop=False)
                    ins = m(o, max_lo[:, t:t + 1], ident_b[0:TILE, 0:TILE], start=False, stop=True)
                ins.then_inc(maxrow_ready, 1)

            def x2_transposed(tau):
                pe.wait_ge(x2_ready, tau.at(3, 1, 1))
                if tau.has(0):
                    pe.wait_ge(h_ready, tau.at(0, 1, 1))
                else:
                    pe.wait_ge(count_read, tau.at(3))
                r = row[tau.slot(3, ROWS)]
                tiles_transposed(lambda t: r[:, t, XN0:XN0 + D], lambda t: WA[:, t * TILE:(t + 1) * TILE],
                                 TILE).then_inc(x2T_ready, 1)

            def logits(tau):
                pe.wait_ge(x2T_copied, tau.at(3, 1, 1))
                for t in range(NT):
                    ins = m(WA[0:TILE, t * E:(t + 1) * E], x2T[:, t * TILE:(t + 1) * TILE], swT[:, :], start=True, stop=True)
                ins.then_inc(logits_ready, 1)

            def counts(tau):
                pe.wait_ge(hot_ready, tau.at(3, 1, 1))
                pe.wait_ge(consts, 10)
                pe.wait_ge(rel_ready, tau.at(3, 1, 1))
                flat = hot[:, :, :].rearrange("p t c -> p (t c)")
                m(WA[0:TILE, 0:(NT + 1) * E], tri[:, :], flat, start=True, stop=False)
                for n in range(1, NT + 1):
                    ins = m(WA[0:TILE, n * E:(NT + 1) * E], ones_b[:, :], flat[:, 0:(NT + 1 - n) * E], start=False, stop=(n == NT))
                ins.then_inc(count_ready, 1)

            parts = ((conv_hi, x_hi), (conv_hi, x_lo), (conv_lo, x_hi))

            def conv(tau, products):
                if not tau.has(0):
                    return
                for n in products:
                    j, (w, xx) = n // 3, parts[n % 3]
                    if tau.first() and n % 6 == 0:
                        setup_parts[n // 6]()
                    if n == 0:
                        if tau.first():
                            pe.wait_ge(su_ev, marks["conv"])
                        pe.wait_ge(xhi_ready, tau.at(0, 1, 1))
                        pe.wait_ge(xlo_ready, tau.at(0, 1, 1))
                        wait(pe, shiftrow_ready, tau.at(1))
                    ins = m(WB[:, 0:COLS], w[:, j * D:(j + 1) * D], xx[:, :, 2 * j:2 * j + SLOTS],
                            start=(n == 0), stop=(n == 3 * PAIRS - 1))
                if products[-1] == 3 * PAIRS - 1:
                    ins.then_inc(conv_ready, 1)

            def step(tau):
                first, second = range(NC // 2), range(NC // 2, NC)

                def maxes(ks):
                    if tau.has(1):
                        max_pass(tau, ks)

                def pv(t, js):
                    if tau.has(2):
                        p_times_v(tau, t, js)

                def scores(j):
                    if tau.has(1):
                        score(tau, j)

                def late_score(j):
                    if tau.has(2):
                        score(tau, j, 2)

                draining = not tau.has(0) and tau.has(1)
                conv(tau, range(0, 8))
                late_score(EARLY)
                maxes((0, 1))
                late_score(EARLY + 1)
                conv(tau, range(8, 11))
                for k in range(2, 2 * NT):
                    maxes((k,))
                    conv(tau, range(2 * k + 7, 2 * k + 9))
                    if draining and k % 4 == 3:
                        pv(k // 4, range(NC))
                conv(tau, range(3 * PAIRS - 1, 3 * PAIRS))
                if not draining:
                    pv(0, range(NC))
                if tau.has(0):
                    pe.wait_ge(hT_ready, tau.at(0, 1, 1))
                    wait(pe, count_read, tau.at(4, 1, 1))
                    tiles_transposed(lambda t: hT[:, t * TILE:(t + 1) * TILE], lambda t: WA[0:TILE, t * D:(t + 1) * D],
                                     128).then_inc(htok_ready, 1)
                if tau.first():
                    setup_values()
                if tau.has(1):
                    max_row(tau)
                if tau.has(-1):
                    if not tau.has(1):
                        wait(pe, xlo_ready, tau.at(0, 1, 1))
                    x_transposed(tau, -1)
                if not draining:
                    pv(1, first)
                scores(0)
                if not draining:
                    pv(1, second)
                scores(1)
                if tau.has(3):
                    x2_transposed(tau)
                pv(2, first)
                scores(2)
                pv(2, second)
                scores(3)
                if tau.has(3):
                    logits(tau)
                pv(3, first)
                if tau.has(0):
                    pe.wait_ge(xn_ready, tau.at(0, 1, 1))
                    tiles_transposed(lambda t: xn[:, t, :], lambda t: XNB[:, t * TILE:(t + 1) * TILE],
                                     TILE).then_inc(xnT_ready, 1)
                scores(4)
                pv(3, second)
                if tau.has(3):
                    counts(tau)
                scores(5)

            x_transposed(Tau(None, 0), 0)
            pipeline(pe, step, {GROUPS + 3: expert_matrices})

            pe.wait_ge(ewlo_ready, 4)

            def expert_products(i):
                for k in range(2):
                    wait(pe, exlo_ready, i * 6 + k * 3)
                    for q in range(3):
                        pe.wait_ge(ld_ex[k][q], i * 16 + 16)
                        for t in range(3):
                            ins = tp(bank[q][:, t * 128:(t + 1) * 128], ex[k][:, q * 3 + t, XN0:XN0 + D], ident[:, :])
                        ins.then_inc(exT_ready, 1)
                    wait(pe, ey_read, i * 6 + k * 3)
                    for q in range(3):
                        pe.wait_ge(exlo_ready, i * 6 + (k * 3 + q + 1))
                        for t in range(3):
                            rows = slice((q * 3 + t) * 128, (q * 3 + t + 1) * 128)
                            o = bank[3 + q][:, t * 128:(t + 1) * 128]
                            w = bass.ds(i * (2 * D) + k * D, D)
                            m(o, exT_hi[:, rows], ew_hi[:, w], start=True, stop=False)
                            m(o, exT_lo[:, rows], ew_hi[:, w], start=False, stop=False)
                            ins = m(o, exT_hi[:, rows], ew_lo[:, w], start=False, stop=True)
                        ins.then_inc(ey_ready, 1)

            expert_pairs(pe, expert_products)


_INS = ["x", "L0_tok_W0", "L0_tok_b0", "L0_tok_W1", "L0_tok_b1", "L0_tok_W2", "L0_tok_b2", "L0_tok_pos",
        "L0_attn_context_embed", "L0_attn_Wq", "L0_attn_bq", "L0_attn_Wk", "L0_attn_bk", "L0_attn_Wv", "L0_attn_bv",
        "L0_attn_Wo", "L0_attn_bo", "L0_ffn_switch_w", "L0_ffn_switch_b", "L0_ffn_expert_w", "L0_ffn_expert_b"]


def kernel(**inputs):
    import numpy as np
    import concourse.bacc as bacc
    from concourse.bass_utils import run_bass_kernel_spmd

    nc = bacc.Bacc("TRN2", target_bir_lowering=False, num_devices=1)
    arrays, args = {}, []
    for name in _INS:
        a = np.ascontiguousarray(inputs[name])
        arrays[f"in_{name}"] = a
        args.append(nc.dram_tensor(f"in_{name}", a.shape, mybir.dt.from_np(a.dtype), kind="ExternalInput").ap())
    args.append(nc.dram_tensor("out", (BATCH, LEN, D), mybir.dt.float32, kind="ExternalOutput").ap())
    build(nc, *args)
    return run_bass_kernel_spmd(nc, [arrays], core_ids=[0]).results[0]["out"]
```
